# Optimizing a Trainium2 kernel written in Bass

```python
import numpy as np
import jax
import jax.numpy as jnp

def _softmax(x, axis=-1):
    return jax.nn.softmax(x, axis=axis)
def _gelu(x):
    return jax.nn.gelu(x, approximate=True)
def _silu(x):
    return jax.nn.silu(x)
def _sigmoid(x):
    return jax.nn.sigmoid(x)
def _layernorm(x, axis=-1, eps=1e-5):
    m = jnp.mean(x, axis=axis, keepdims=True)
    v = jnp.var(x, axis=axis, keepdims=True)
    return (x - m) / jnp.sqrt(v + eps)
def _scatter_add(tgt, idx, src, axis=0):
    return tgt.at[idx].add(src)
def _segment_sum(src, seg, n):
    return jax.ops.segment_sum(src, seg, n)

kernel_name = 'mk_conv_preact_d2_conv_nchw64_1d9f4f'

def setup_inputs(seed: int = 0):
    np.random.seed(seed)
    _w = jnp.asarray
    def _rec_inputs():
        import jax
        import jax.numpy as jnp
        _gk = jax.random.key(seed)
        x = -0.0003929 + 0.9999 * jax.random.normal(jax.random.fold_in(_gk, 1), (16, 64, 128, 128), jnp.float32)
        return x
    x = _rec_inputs()
    def _L0_conv_setup():
        import jax, jax.numpy as jnp
        import numpy as np
        IN_CH, OUT_CH, K, LAYERS = (64, 64, 4, 3)
        DIMS = 16

        def _gate_positions(num_qubits, num_layers):
            pos = []
            for layer in range(num_layers * 2):
                q = layer % 2
                while q + 1 < num_qubits:
                    pos.append((q, q + 1))
                    q += 2
            return pos
        GATE_POS = _gate_positions(DIMS, LAYERS)
        NUM_GATES = len(GATE_POS)

        def _synthesize_weight(gates):
            state = jnp.zeros((2,) * DIMS, dtype=gates.dtype).at[(0,) * DIMS].set(1.0)
            ndim = DIMS
            for n, (p0, p1) in enumerate(GATE_POS):
                state = jnp.tensordot(state, gates[n], axes=[[p0, p1], [0, 1]])
                order = list(range(p0)) + [ndim - 2] + list(range(p0, p1 - 1)) + [ndim - 1] + list(range(p1 - 1, ndim - 2))
                state = jnp.transpose(state, order)
                if (n + 1) % (ndim - 1) == 0 and (n + 1) // (ndim - 1) < NUM_GATES / (ndim - 1):
                    state = jax.nn.relu(state)
            return state.reshape(OUT_CH, IN_CH, K, K)
        key = jax.random.key(seed)
        k1, k2 = jax.random.split(key)
        x = jax.random.normal(k1, (16, IN_CH, 128, 128), dtype=jnp.float32)
        eye = jnp.eye(4, dtype=jnp.float32)
        gates = eye[None] + 0.1 * jax.random.normal(k2, (NUM_GATES, 4, 4), dtype=jnp.float32)
        gates = gates.reshape(NUM_GATES, 2, 2, 2, 2)
        return {'x': x, 'gates': gates}
    _L0_conv_all = _L0_conv_setup()
    _L0_conv_in = {k: v for k, v in _L0_conv_all.items() if k in ('gates', )}
    del _L0_conv_all

    def _L1_conv_setup():
        import jax, jax.numpy as jnp
        import numpy as np
        from jax import lax
        B, DIM, H, W = (4, 64, 256, 256)
        HID = int(DIM * 3)
        P = 16

        def _conv(x, w, pad, groups):
            return lax.conv_general_dilated(x, w, window_strides=(1, 1), padding=[(pad, pad), (pad, pad)], dimension_numbers=('NCHW', 'OIHW', 'NCHW'), feature_group_count=groups)
        key = jax.random.key(seed)
        ks = jax.random.split(key, 7)
        x = jax.random.normal(ks[0], (B, DIM, H, W), dtype=jnp.float32)
        w_in = jax.random.normal(ks[1], (HID, DIM, 1, 1), dtype=jnp.float32) * 0.05
        fft_w = jnp.ones((HID, 1, 1, P, P // 2 + 1), dtype=jnp.float32)
        w1 = jax.random.normal(ks[2], (HID, 1, 1, 1), dtype=jnp.float32) * 0.05
        w3 = jax.random.normal(ks[3], (HID, 1, 3, 3), dtype=jnp.float32) * 0.05
        w5 = jax.random.normal(ks[4], (HID, 1, 5, 5), dtype=jnp.float32) * 0.05
        w_out = jax.random.normal(ks[5], (DIM, HID * 3, 1, 1), dtype=jnp.float32) * 0.05
        return {'x': x, 'w_in': w_in, 'fft_w': fft_w, 'w1': w1, 'w3': w3, 'w5': w5, 'w_out': w_out}
    _L1_conv_all = _L1_conv_setup()
    _L1_conv_in = {k: v for k, v in _L1_conv_all.items() if k in ('w_in', 'fft_w', 'w1', 'w3', 'w5', 'w_out', )}
    del _L1_conv_all

    return {
        "x": x,
        "L0_conv_gates": _L0_conv_in["gates"],
        "L1_conv_w_in": _L1_conv_in["w_in"],
        "L1_conv_fft_w": _L1_conv_in["fft_w"],
        "L1_conv_w1": _L1_conv_in["w1"],
        "L1_conv_w3": _L1_conv_in["w3"],
        "L1_conv_w5": _L1_conv_in["w5"],
        "L1_conv_w_out": _L1_conv_in["w_out"],
    }

def reference(x, L0_conv_gates, L1_conv_w_in, L1_conv_fft_w, L1_conv_w1, L1_conv_w3, L1_conv_w5, L1_conv_w_out):
    import jax
    import jax.numpy as jnp
    def _L0_conv_ref(x, gates):
        import jax, jax.numpy as jnp
        import numpy as np
        IN_CH, OUT_CH, K, LAYERS = (64, 64, 4, 3)
        DIMS = 16

        def _gate_positions(num_qubits, num_layers):
            pos = []
            for layer in range(num_layers * 2):
                q = layer % 2
                while q + 1 < num_qubits:
                    pos.append((q, q + 1))
                    q += 2
            return pos
        GATE_POS = _gate_positions(DIMS, LAYERS)
        NUM_GATES = len(GATE_POS)

        def _synthesize_weight(gates):
            state = jnp.zeros((2,) * DIMS, dtype=gates.dtype).at[(0,) * DIMS].set(1.0)
            ndim = DIMS
            for n, (p0, p1) in enumerate(GATE_POS):
                state = jnp.tensordot(state, gates[n], axes=[[p0, p1], [0, 1]])
                order = list(range(p0)) + [ndim - 2] + list(range(p0, p1 - 1)) + [ndim - 1] + list(range(p1 - 1, ndim - 2))
                state = jnp.transpose(state, order)
                if (n + 1) % (ndim - 1) == 0 and (n + 1) // (ndim - 1) < NUM_GATES / (ndim - 1):
                    state = jax.nn.relu(state)
            return state.reshape(OUT_CH, IN_CH, K, K)
        n, c, h, w = x.shape
        g = c // 4
        x1 = jnp.pad(x[:, 0 * g:1 * g], ((0, 0), (0, 0), (1, 0), (1, 0)))
        x2 = jnp.pad(x[:, 1 * g:2 * g], ((0, 0), (0, 0), (1, 0), (0, 1)))
        x3 = jnp.pad(x[:, 2 * g:3 * g], ((0, 0), (0, 0), (0, 1), (1, 0)))
        x4 = jnp.pad(x[:, 3 * g:4 * g], ((0, 0), (0, 0), (0, 1), (0, 1)))
        xp = jnp.concatenate([x1, x2, x3, x4], axis=1)
        w_conv = _synthesize_weight(gates)
        pad = (K - 2) // 2
        return jax.lax.conv_general_dilated(xp, w_conv, window_strides=(1, 1), padding=[(pad, pad), (pad, pad)], dimension_numbers=('NCHW', 'OIHW', 'NCHW'))

    def _L1_conv_ref(x, w_in, fft_w, w1, w3, w5, w_out):
        import jax, jax.numpy as jnp
        import numpy as np
        from jax import lax
        B, DIM, H, W = (4, 64, 256, 256)
        HID = int(DIM * 3)
        P = 16

        def _conv(x, w, pad, groups):
            return lax.conv_general_dilated(x, w, window_strides=(1, 1), padding=[(pad, pad), (pad, pad)], dimension_numbers=('NCHW', 'OIHW', 'NCHW'), feature_group_count=groups)
        x = _conv(x, w_in, 0, 1)
        b, c, h, w = x.shape
        hp, wp = (h // P, w // P)
        xp = x.reshape(b, c, hp, P, wp, P).transpose(0, 1, 2, 4, 3, 5)
        xf = jnp.fft.rfft2(xp.astype(jnp.float32))
        xf = xf * fft_w
        xp = jnp.fft.irfft2(xf, s=(P, P))
        x = xp.transpose(0, 1, 2, 4, 3, 5).reshape(b, c, h, w)
        x1 = _conv(x, w1, 0, c)
        x3 = _conv(x, w3, 1, c)
        x5 = _conv(x, w5, 2, c)
        g = jax.nn.gelu(x1, approximate=False)
        gate1 = g * x3
        gate2 = g * x5
        out = _conv(jnp.concatenate([gate1, gate2, x1], axis=1), w_out, 0, 1)
        return out

    def _gn(v, G=32, eps=1e-5):
        B_, C_, H_, W_ = v.shape
        g = v.reshape(B_, G, C_ // G, H_, W_)
        m = jnp.mean(g, axis=(2, 3, 4), keepdims=True)
        s = jnp.var(g, axis=(2, 3, 4), keepdims=True)
        return ((g - m) / jnp.sqrt(s + eps)).reshape(v.shape)

    def _ln_c(v, eps=1e-6):
        m = jnp.mean(v, axis=1, keepdims=True)
        s = jnp.var(v, axis=1, keepdims=True)
        return (v - m) / jnp.sqrt(s + eps)

    def _ln_t(v, eps=1e-5):
        m = jnp.mean(v, axis=-1, keepdims=True)
        s = jnp.var(v, axis=-1, keepdims=True)
        return (v - m) / jnp.sqrt(s + eps)

    def _to_tokens(v):
        B_, C_, H_, W_ = v.shape
        return v.reshape(B_, C_, H_ * W_).transpose(0, 2, 1)
    def _from_tokens(t, like):
        B_, C_, H_, W_ = like.shape
        return t.transpose(0, 2, 1).reshape(B_, C_, H_, W_)

    x = x + _L0_conv_ref(_gn(x), L0_conv_gates)
    x = x + _L1_conv_ref(_gn(x), L1_conv_w_in, L1_conv_fft_w, L1_conv_w1, L1_conv_w3, L1_conv_w5, L1_conv_w_out)
    return x


_drawn_inputs = setup_inputs


def setup_inputs(seed=0):
    import zlib

    import numpy as np

    out = dict(_drawn_inputs(seed))
    spreads = {'L1_conv_fft_w': (1.0, 0.6)}
    factors = {'L1_conv_w_in': 3.819,
     'L1_conv_w1': 3.88,
     'L1_conv_w3': 8.0,
     'L1_conv_w5': 8.0,
     'L1_conv_w_out': 3.853}
    for name, (base, spread) in spreads.items():
        noise = np.random.default_rng([zlib.crc32(name.encode()), seed]).standard_normal(out[name].shape)
        drawn = base * np.exp(spread * noise) if base else spread * noise
        out[name] = jnp.asarray(drawn.astype(out[name].dtype))
    for name, factor in factors.items():
        out[name] = (out[name] * factor).astype(out[name].dtype)
    return out
```

```python
from contextlib import ExitStack

import concourse.bass as bass
import numpy as np
from concourse import mybir

F32 = mybir.dt.float32
F16 = mybir.dt.float16
ALU = mybir.AluOpType
ACT = mybir.ActivationFunctionType

P = 128
C = 64
HW = 128
RP = HW // 2
HID = 192
KC = HID // C
EPS = 1e-5
FR_W = 132
XS_W = 130
CH = 16
TP = 33
HALF = 16 * TP
Y1W = 1124
Y2W = 1092
GN_ = 33 * TP
GW = 1090
NB = GN_ // 3
NG = HID // 8
SLOTS = 8
OPEN = 1
CREDIT = 2
SPLITS = ((0, 0), (0, 1), (1, 0))


def view(ap, off, dims, parts=None, p0=0):
    step = ap.ap[0][0]
    n = ap.ap[0][1] if parts is None else parts
    return bass.AP(tensor=ap.tensor, offset=ap.offset + p0 * step + off, ap=[[step, n]] + [list(d) for d in dims])


def dram(ap, off, dims):
    return bass.AP(tensor=ap.tensor, offset=ap.offset + off, ap=[list(d) for d in dims])


def pairs(eng, N):
    if N > 2:
        with eng.Fori(0, N // 2 - 1) as j:
            yield j


def stage0(nc, a):
    ctx = ExitStack()
    with ctx:
        def sb(name, shape, dt=F32):
            return ctx.enter_context(nc.sbuf_tensor(name, shape, dt))

        def sem(name):
            return ctx.enter_context(nc.semaphore(name))

        ge = sb("ge", [P, 3, 2, 2, 4, 4])
        go = sb("go", [P, 3, 6, 4])
        gx = sb("gx", [P, 3, 4, 2])
        i2 = sb("i2", [P, 2])
        K = sb("K", [P, 2, 2, 256])
        R = sb("R", [P, 4, 128])
        Cm = sb("Cm", [P, 128])
        o16 = sb("o16", [P, 2, 16])
        o64 = sb("o64", [P, 2, 64])
        S = sb("S", [P, 2, 256])
        T = sb("T", [P, 2, 256])
        Wo = sb("Wo", [C, 1024])
        Wt = sb("Wt", [C, 12, 2, 2, 2, 2, 16])
        tab = sb("tab", [P, NG, 128])
        cmask = sb("cmask", [P, 8])
        W32 = sb("W32", [P, 2, 1024])
        Whl = sb("Whl", [P, 2, 2, 1024], F16)
        zero = sb("zero", [P, 96 * 36], F16)
        win32 = sb("win32", [P, KC, 128])
        wout32 = sb("wout32", [P, KC, 128])
        wg32 = sb("wg32", [P, KC, 64])
        w1c = sb("w1c", [P, KC])
        fw = sb("fw", [P, 2, 2, HID])
        psT = ctx.enter_context(nc.psum_tensor("psT", [P, 2, 256], F32))
        psS = ctx.enter_context(nc.psum_tensor("psS", [P, 2, 256], F32))
        psW = ctx.enter_context(nc.psum_tensor("psW", [P, 12, 128], F32))

        gates_in = sem("gates_in")
        consts_in = sem("consts_in")
        blocks_in = sem("blocks_in")
        zeroed = sem("zeroed")
        step = sem("dve_step")
        mats = sem("mats_built")
        pe_step = sem("pe_step")
        ev = sem("state_evacuated")
        s_out = sem("state_stored")
        s_in = sem("weight_loaded")
        wt_done = sem("taps_laid_out")
        wtr = sem("taps_transposed")
        whi = sem("conv_weight_hi")
        w32 = sem("band_built")
        bhi = sem("band_hi")
        blo = sem("band_lo")
        bst = [sem("band_stored0"), sem("band_stored1")]
        zst = sem("frames_zeroed")
        cst = sem("const_hi")
        n_gates, n_consts, n_blocks = 4, 11, 8

        block = ctx.enter_context(nc.Block())

        @block.sync
        def _(sp):
            sp.dma_start(ge[:], a["ge"]).then_inc(gates_in, 16)
            sp.dma_start(go[:], a["go"]).then_inc(gates_in, 16)
            sp.dma_start(gx[:], a["gx"]).then_inc(gates_in, 16)
            sp.dma_start(i2[:], a["i2"]).then_inc(gates_in, 16)
            sp.dma_start(a["ident"][:], a["d_ident"]).then_inc(consts_in, 16)
            sp.dma_start(a["gmask"][:], a["d_gmask"]).then_inc(consts_in, 16)
            sp.dma_start(tab[:], a["tab"]).then_inc(consts_in, 16)
            sp.dma_start(cmask[:], a["cmask"]).then_inc(consts_in, 16)
            sp.dma_start(a["Bf"][:], a["d_Bf"]).then_inc(consts_in, 16)
            sp.dma_start(a["Bi"][:], a["d_Bi"]).then_inc(consts_in, 16)
            sp.dma_start(fw[:], a["fw"]).then_inc(consts_in, 16)
            sp.dma_start(a["w1g"][:], a["d_w1g"]).then_inc(consts_in, 16)
            sp.dma_start(w1c[:], a["w1c"]).then_inc(consts_in, 16)
            for t in range(2):
                sp.dma_start(view(wg32[:], 0, [[64, KC], [1, 64]], C, C * t),
                             dram(a["wout"], t * HID * C, [[C, C], [C * C, KC], [1, C]])).then_inc(consts_in, 16)
            sp.wait_ge(zeroed, 2)
            for h in range(2):
                for k in range(KC):
                    sp.dma_start(view(win32[:], k * 128 + C * h, [[1, C]], C, C * h),
                                 dram(a["win"], k * C, [[HID, C], [1, C]])).then_inc(blocks_in, 16)
                sp.dma_start(view(wout32[:], C * h, [[128, KC], [1, 64]], C, C * h),
                             dram(a["wout"], 2 * HID * C, [[C, C], [C * C, KC], [1, C]])).then_inc(blocks_in, 16)
            sp.wait_ge(zeroed, 3)
            rows = HID * 32 // 64
            for name, width, tail in (("Y1", Y1W, 34), ("Y2", Y2W, 36)):
                for off in (0, width - tail):
                    sp.dma_start(dram(a[name], off, [[width * rows, 64], [width, rows], [1, tail]]),
                                 view(zero[:], 0, [[tail, rows], [1, tail]], 64)).then_inc(zst, 16)
            sp.wait_ge(ev, 13)
            sp.dma_start(dram(a["ws"], 0, [[256, P], [P * 256, 2], [1, 256]]), S[:]).then_inc(s_out, 16)
            sp.wait_ge(s_out, 16)
            for u in range(2):
                for t in range(2):
                    sp.dma_start(view(Wo[:], 0, [[1, 1024]], 16, 32 * u + 16 * t),
                                 dram(a["ws"], (32 * t + 16 * u) * 1024, [[1024, 16], [1, 1024]])).then_inc(s_in, 16)
            sp.wait_ge(zst, 64)
            sp.wait_ge(bst[0], OPEN + 16 * NG // 2)
            sp.wait_ge(bst[1], OPEN + 16 * NG // 2)

        @block.gpsimd
        def _(pool):
            nc.gpsimd.memset(win32[:], 0.0).then_inc(zeroed, 1)
            nc.gpsimd.memset(wout32[:], 0.0).then_inc(zeroed, 1)
            nc.gpsimd.memset(zero[:], 0.0).then_inc(zeroed, 1)
            with pool.Fori(0, NG // 2) as j:
                for p in range(2):
                    pool.wait_ge(bhi, j * 2 + p + 1)
                    nc.gpsimd.tensor_tensor(Whl[:, p, 1, :], W32[:, p, :], Whl[:, p, 0, :], ALU.subtract).then_inc(blo, 1)

        @block.vector
        def _(dve):
            n = [0]

            def link(ins):
                n[0] += 1
                ins.then_inc(step, 1)
                dve.wait_ge(step, n[0])

            def outer(out, off, x, xoff, y, yoff, nx, ny, outs=None):
                so, sx, sy, b = outs or (0, 0, 0, 1)
                return nc.vector.tensor_tensor(view(out[:], off, [[so, b], [ny, nx], [1, ny]]),
                                               view(x[:], xoff, [[sx, b], [1, nx], [0, ny]]),
                                               view(y[:], yoff, [[sy, b], [0, nx], [1, ny]]), ALU.mult)

            link(nc.vector.memset(S[:], 0.0))
            nc.vector.memset(S[0:1, 0, 0:1], 1.0).then_inc(ev, 1)
            link(nc.vector.memset(Wt[:], 0.0))
            dve.wait_ge(gates_in, 16 * n_gates)
            for r in range(3):
                if r:
                    dve.wait_ge(pe_step, 4 * r)
                for op in range(2):
                    g0 = (r * 2 + op) * 32
                    link(outer(o16, 0, ge, g0, ge, g0 + 4, 4, 4, (16, 16, 16, 2)))
                    link(outer(o64, 0, o16, 0, ge, g0 + 8, 16, 4, (64, 16, 16, 2)))
                    outer(K, op * 512, o64, 0, ge, g0 + 12, 64, 4, (256, 64, 16, 2)).then_inc(mats, 1)
                    dve.wait_ge(mats, 4 * r + op + 1)
                g0 = r * 24
                link(outer(o16, 0, go, g0, go, g0 + 4, 4, 4))
                link(outer(o64, 0, o16, 0, go, g0 + 8, 16, 4))
                outer(R, 0, o64, 0, gx, r * 8, 64, 2, (128, 0, 2, 4)).then_inc(mats, 1)
                dve.wait_ge(mats, 4 * r + 3)
                link(outer(o16, 0, go, g0 + 12, go, g0 + 16, 4, 4))
                link(outer(o64, 0, o16, 0, go, g0 + 20, 16, 4))
                outer(Cm, 0, o64, 0, i2, 0, 64, 2).then_inc(mats, 1)
                for q, (dst, src) in enumerate(((T, psT), (S, psS), (T, psT), (S, psS))):
                    dve.wait_ge(pe_step, 4 * r + q + 1)
                    if q == 3 and r < 2:
                        nc.vector.tensor_scalar(dst[:], src[:], 0.0, None, ALU.max).then_inc(ev, 1)
                    else:
                        nc.vector.tensor_copy(dst[:], src[:]).then_inc(ev, 1)
            dve.wait_ge(consts_in, 16 * n_consts)
            dve.wait_ge(blocks_in, 16 * n_blocks)
            link(nc.vector.tensor_tensor(fw[:, :, 0, :], fw[:, :, 0, :], fw[:, :, 1, :], ALU.add))
            nc.vector.tensor_scalar(a["wf"][:], fw[:, :, 0, :], 0.5 / 16, None, ALU.mult).then_inc(cst, 1)
            for k in range(KC):
                link(nc.vector.tensor_scalar(wout32[:, k, :], wout32[:, k, :], w1c[:, k:k + 1], None, ALU.mult))
            for t32, hl in ((win32, a["Win"]), (wout32, a["W3"]), (wg32, a["Wg"])):
                link(nc.vector.tensor_copy(hl[:, 0], t32[:]))
                nc.vector.tensor_tensor(hl[:, 1], t32[:], hl[:, 0], ALU.subtract).then_inc(cst, 1)
            with dve.Fori(0, NG // 2) as j:
                for p in range(2):
                    dve.wait_ge(bst[p], OPEN + 16 * j)
                    nc.vector.tensor_tensor(view(W32[:], p * 1024, [[128, 8], [16, 8], [1, 16]]),
                                            view(tab[:], (j * 2 + p) * 128, [[16, 8], [0, 8], [1, 16]]),
                                            view(cmask[:], 0, [[0, 8], [1, 8], [0, 16]]), ALU.mult).then_inc(w32, 1)
            dve.wait_ge(s_in, 64)
            for si in range(3):
                for po in range(2):
                    for pi in range(2):
                        for t in range(2):
                            kh = 2 * (si - 1) + pi - po + 2 - t
                            if 0 <= kh < 4:
                                last = nc.vector.tensor_copy(
                                    view(Wt[:], si * 1024 + po * 128 + pi * 64 + t * 16, [[256, 4], [32, 2], [1, 16]]),
                                    view(Wo[:], t * 32 * 16 + kh * 4, [[1, 4], [256, 2], [16, 16]]))
            last.then_inc(wt_done, 1)
            dve.wait_ge(whi, 1)
            nc.vector.tensor_tensor(a["Wc"][:, 1], psW[:], a["Wc"][:, 0], ALU.subtract).then_inc(cst, 1)

        @block.scalar
        def _(act):
            act.sem_inc(bst[0], OPEN)
            act.sem_inc(bst[1], OPEN)
            with act.Fori(0, NG // 2) as j:
                for p in range(2):
                    act.wait_ge(w32, j * 2 + p + 1)
                    nc.scalar.activation(Whl[:, p, 0, :], W32[:, p, :], ACT.Copy).then_inc(bhi, 1)
                    act.wait_ge(blo, j * 2 + p + 1)
                    act.dma_start(dram(a["Cw"], (j * 2 + p) * P * 2048, [[2048, P], [1, 2048]]),
                                  view(Whl[:], p * 2048, [[1, 2048]])).then_inc(bst[p], 16)
            act.wait_ge(wtr, 1)
            nc.scalar.activation(a["Wc"][:, 0], psW[:], ACT.Copy).then_inc(whi, 1)

        @block.tensor
        def _(pe):
            for r in range(3):
                for q in range(4):
                    pe.wait_ge(ev, 4 * r + q + 1)
                    pe.wait_ge(mats, 4 * r + q + 1)
                    if q < 2:
                        src, dst = (S, psT) if q == 0 else (T, psS)
                        for m in range(2):
                            for kb in range(2):
                                last = nc.tensor.matmul(dst[:, m, :], src[:, kb, m * 128:(m + 1) * 128], K[:, q, kb, :],
                                                        start=(kb == 0), stop=(kb == 1))
                    elif q == 2:
                        for bo in range(2):
                            for kb in range(2):
                                for b in range(2):
                                    last = nc.tensor.matmul(psT[:, bo, kb * 128:(kb + 1) * 128],
                                                            S[:, kb, b * 128:(b + 1) * 128], R[:, 2 * b + bo, :],
                                                            start=(b == 0), stop=(b == 1))
                    else:
                        for m in range(2):
                            for cb in range(2):
                                last = nc.tensor.matmul(psS[:, m, cb * 128:(cb + 1) * 128],
                                                        T[:, cb, m * 128:(m + 1) * 128], Cm[:], start=True, stop=True)
                    last.then_inc(pe_step, 1)
            pe.wait_ge(wt_done, 1)
            pe.wait_ge(consts_in, 16 * n_consts)
            for tk in range(12):
                for po in range(2):
                    last = nc.tensor.matmul(psW[:, tk, po * C:(po + 1) * C],
                                            view(Wt[:], tk * 256 + po * 128, [[1, 128]]),
                                            a["ident"][0:C, 0:C], start=True, stop=True, is_transpose=True)
            last.then_inc(wtr, 1)


def stage1(nc, a, N):
    ctx = ExitStack()
    with ctx:
        def sb(name, shape, dt=F32):
            return ctx.enter_context(nc.sbuf_tensor(name, shape, dt))

        def sem(name):
            return ctx.enter_context(nc.semaphore(name))

        raw = sb("raw", [P, RP, XS_W])
        img = [sb(f"img{b}", [P, RP, HW]) for b in range(2)]
        xn = [sb(f"xn{b}", [P, 2, RP + 2, FR_W], F16) for b in range(2)]
        st1 = sb("st1", [P, CH, 6])
        st2 = sb("st2", [P, CH, 6])
        mv = sb("mv", [P, 2])
        tmp = sb("tmp", [P, 4])
        sd = sb("sd", [P, 1])
        co = sb("co", [P, 2])
        zcol = sb("zcol", [P, 16, 1])
        psC = ctx.enter_context(nc.psum_tensor("psC", [P, 2, 512], F32))
        psG = ctx.enter_context(nc.psum_tensor("psG", [P, 2], F32))

        img_in = [sem("img_in0"), sem("img_in1")]
        raw_in = sem("raw_in")
        img_out = [sem("img_out0"), sem("img_out1")]
        pads = sem("frames_cleared")
        step = sem("dve_step1")
        mom = sem("moments_ready")
        gsum = sem("group_sums")
        vready = sem("variance_ready")
        root = sem("root_ready")
        coef = sem("norm_coef")
        n32 = sem("normed_f32")
        nhi = sem("normed_hi")
        lows = sem("low_halves")
        nlo = sem("normed_lo")
        taken = sem("stats_taken")
        conv = sem("conv_done")
        added = sem("residual_added")

        block = ctx.enter_context(nc.Block())
        xi, xs = a["x"], a["xs"]
        IM = C * HW * HW

        def load_img(eng, n, b):
            for par in range(2):
                eng.dma_start(view(img[b][:], 0, [[HW, RP], [1, HW]], C, C * par),
                              dram(xi, n * IM + par * HW, [[HW * HW, C], [2 * HW, RP], [1, HW]])).then_inc(img_in[b], 16)

        def load_raw(eng, n):
            for par in range(2):
                for u in range(2):
                    eng.dma_start(view(raw[:], 1 - u, [[XS_W, RP], [1, HW]], 32, C * par + 32 * u),
                                  dram(xi, n * IM + u * 32 * HW * HW + par * HW,
                                       [[HW * HW, 32], [2 * HW, RP], [1, HW]])).then_inc(raw_in, 16)

        @block.sync
        def _(sp):
            sp.sem_inc(img_out[0], OPEN)
            sp.sem_inc(img_out[1], OPEN)
            def prep(n, b, m):
                sp.wait_ge(img_out[b], OPEN + m * 32)
                if not isinstance(n, int) or n:
                    sp.wait_ge(mom, 2 * n - 1)
                load_img(sp, n, b)
                sp.wait_ge(nlo, OPEN + n * 4)
                load_raw(sp, n)

            def post(n, b):
                sp.wait_ge(added, n * CH + CH + CREDIT)
                for par in range(2):
                    sp.dma_start(dram(xs, n * IM + par * HW, [[HW * HW, C], [2 * HW, RP], [1, HW]]),
                                 view(img[b][:], 0, [[HW, RP], [1, HW]], C, C * par)).then_inc(img_out[b], 16)

            sp.wait_ge(pads, 4)
            prep(0, 0, 0)
            for j in pairs(sp, N):
                prep(2 * j + 1, 1, j)
                post(2 * j, 0)
                prep(2 * j + 2, 0, j + 1)
                post(2 * j + 1, 1)
            prep(N - 1, 1, N // 2 - 1)
            post(N - 2, 0)
            post(N - 1, 1)
            sp.wait_ge(img_out[0], OPEN + 32 * (N // 2))
            sp.wait_ge(img_out[1], OPEN + 32 * (N // 2))

        @block.gpsimd
        def _(pool):
            pool.sem_inc(nlo, OPEN)
            nc.gpsimd.memset(raw[:], 0.0).then_inc(pads, 1)
            nc.gpsimd.memset(xn[0][:], 0.0).then_inc(pads, 1)
            nc.gpsimd.memset(xn[1][:], 0.0).then_inc(pads, 1)
            nc.gpsimd.memset(zcol[:], 0.0).then_inc(pads, 1)
            pool.wait_ge(pads, 4)

            def prep(n, b):
                for q in range(4):
                    pool.wait_ge(nlo, OPEN + n * 4 + q)
                    pool.wait_ge(nhi, n * 4 + q + 1)
                    rows = slice(16 * q, 16 * q + 16)
                    frame = slice(16 * q + 1, 16 * q + 17)
                    nc.gpsimd.tensor_tensor(xn[b][:, 1, frame, 1:130], raw[:, rows, 0:129], xn[b][:, 0, frame, 1:130],
                                            ALU.subtract).then_inc(lows, 1)
                    pool.wait_ge(lows, n * 4 + q + 1)
                    for part in range(4):
                        col = 1 if part % 2 == 0 else 129
                        edge = slice(32 * part, 32 * part + 32)
                        for border in (raw[edge, rows, col - 1:col], xn[b][edge, 0, frame, col:col + 1], xn[b][edge, 1, frame, col:col + 1]):
                            last = nc.gpsimd.tensor_tensor(border, zcol[edge], zcol[edge], ALU.add)
                    last.then_inc(nlo, 1)

            prep(0, 0)
            for j in pairs(pool, N):
                prep(2 * j + 1, 1)
                prep(2 * j + 2, 0)
            prep(N - 1, 1)

        @block.scalar
        def _(act):
            def sqrt_step(v):
                act.wait_ge(vready, v)
                nc.scalar.activation(sd[:], tmp[:, 0:1], ACT.Sqrt).then_inc(root, 1)

            def prep(n, b, v):
                sqrt_step(v)
                act.wait_ge(coef, n + 1)
                act.wait_ge(raw_in, n * 64 + 64)
                if not isinstance(n, int) or n:
                    act.wait_ge(conv, OPEN + (n - 1) * CH)
                for q in range(4):
                    rows = slice(16 * q, 16 * q + 16)
                    nc.scalar.activation(raw[:, rows, 0:129], raw[:, rows, 0:129], ACT.Identity,
                                         bias=co[:, 1:2], scale=co[:, 0:1]).then_inc(n32, 1)
                    act.wait_ge(n32, n * 4 + q + 1)
                    nc.scalar.activation(xn[b][:, 0, 16 * q + 1:16 * q + 17, 1:130], raw[:, rows, 0:129],
                                         ACT.Copy).then_inc(nhi, 1)

            prep(0, 0, 1)
            for j in pairs(act, N):
                prep(2 * j + 1, 1, j * 4 + 2)
                sqrt_step(j * 4 + 3)
                prep(2 * j + 2, 0, j * 4 + 4)
                sqrt_step(j * 4 + 5)
            prep(N - 1, 1, 2 * N - 2)
            sqrt_step(2 * N - 1)
            sqrt_step(2 * N)

        @block.vector
        def _(dve):
            def link(ins, n):
                ins.then_inc(step, 1)
                dve.wait_ge(step, n)

            LINKS = 9

            def coefs(stats, v, out, done):
                n = (v - 1) * LINKS
                dve.wait_ge(taken, v)
                nc.vector.memset(tmp[:, 3:4], 0.0)
                link(nc.vector.bn_aggr(mv[:], stats[:]), n + 1)
                link(nc.vector.tensor_tensor(tmp[:, 1:2], mv[:, 0:1], mv[:, 0:1], ALU.mult), n + 2)
                nc.vector.tensor_tensor(mv[:, 1:2], mv[:, 1:2], tmp[:, 1:2], ALU.add).then_inc(mom, 1)
                dve.wait_ge(gsum, v)
                link(nc.vector.tensor_copy(mv[:], psG[:]), n + 3)
                link(nc.vector.tensor_tensor(tmp[:, 1:2], mv[:, 0:1], mv[:, 0:1], ALU.mult), n + 4)
                link(nc.vector.tensor_tensor(tmp[:, 0:1], mv[:, 1:2], tmp[:, 1:2], ALU.subtract), n + 5)
                nc.vector.tensor_scalar(tmp[:, 0:1], tmp[:, 0:1], EPS, None, ALU.add).then_inc(vready, 1)
                dve.wait_ge(root, v)
                link(nc.vector.reciprocal(tmp[:, 1:2], sd[:]), n + 6)
                link(nc.vector.scalar_tensor_tensor(tmp[:, 2:3], tmp[:, 1:2], tmp[:, 1:2], tmp[:, 0:1], ALU.mult, ALU.mult), n + 7)
                link(nc.vector.tensor_scalar(tmp[:, 2:3], tmp[:, 2:3], -0.5, 1.5, ALU.mult, ALU.add), n + 8)
                link(nc.vector.tensor_tensor(out(0), tmp[:, 1:2], tmp[:, 2:3], ALU.mult), n + 9)
                last = nc.vector.scalar_tensor_tensor(out(1), mv[:, 0:1], -1.0, out(0), ALU.mult, ALU.mult)
                if done is not None:
                    last.then_inc(done, 1)

            def out1(i):
                return co[:, i:i + 1]

            def stat1(b, c):
                last = nc.vector.bn_stats(st1[:, c, :], img[b][:, 4 * c:4 * c + 4, :].rearrange("p a w -> p (a w)"))
                if c == CH - 1:
                    last.then_inc(taken, 1)

            def add(n, b, c):
                dve.wait_ge(conv, OPEN + n * CH + c + 1)
                rows = img[b][:, 4 * c:4 * c + 4, :].rearrange("p a w -> p (a w)")
                nc.vector.tensor_tensor(rows, psC[:, c % 2, :], rows, ALU.add).then_inc(added, 1)
                dve.wait_ge(added, n * CH + c + 1 + CREDIT)
                last = nc.vector.bn_stats(st2[:, c, :], rows)
                if c == CH - 1:
                    last.then_inc(taken, 1)

            def second(n, v):
                base = stat_ap
                coefs(st2, v, lambda i: view(base, n * 2 + i, [[1, 1]]), None)

            def body(n, b, v, prep=True):
                if prep:
                    dve.wait_ge(img_in[1 - b], 32 * ((n + 1) // 2) + 32)
                for c in range(CH // 2):
                    add(n, b, c)
                    if prep:
                        stat1(1 - b, 2 * c)
                        stat1(1 - b, 2 * c + 1)
                if prep:
                    dve.wait_ge(nlo, OPEN + n * 4 + 4)
                    coefs(st1, v, out1, coef)
                for c in range(CH // 2, CH):
                    add(n, b, c)
                second(n, v + 1 if prep else v)

            stat_ap = a["norm2"][:]
            nc.vector.sem_inc(added, CREDIT)
            dve.wait_ge(img_in[0], 32)
            for c in range(CH):
                stat1(0, c)
            coefs(st1, 1, out1, coef)
            for j in pairs(dve, N):
                body(2 * j, 0, j * 4 + 2)
                body(2 * j + 1, 1, j * 4 + 4)
            body(N - 2, 0, 2 * N - 2)
            body(N - 1, 1, 2 * N, prep=False)

        @block.tensor
        def _(pe):
            pe.sem_inc(conv, OPEN)
            def group_sum(v):
                pe.wait_ge(mom, v)
                nc.tensor.matmul(psG[:], a["gmask"][:], mv[:], start=True, stop=True).then_inc(gsum, 1)

            def chunks(n, b, c0, c1):
                with pe.Fori(c0 // 2, c1 // 2) as h:
                    for p in range(2):
                        c = h * 2 + p
                        pe.wait_ge(nlo, OPEN + n * 4 + 4)
                        pe.wait_ge(added, n * CH + c - 2 + CREDIT + 1)
                        t = 0
                        for si in range(3):
                            for kw in range(4):
                                for wi, di in SPLITS:
                                    last = nc.tensor.matmul(
                                        psC[:, p, :], a["Wc"][:, wi, si * 4 + kw, :],
                                        view(xn[b][:], di * (RP + 2) * FR_W + (c * 4 + si) * FR_W + kw, [[FR_W, 4], [1, HW]]),
                                        start=(t == 0), stop=(t == 35))
                                    t += 1
                        last.then_inc(conv, 1)

            def body(n, b, v, prep=True):
                chunks(n, b, 0, CH // 2)
                if prep:
                    group_sum(v)
                chunks(n, b, CH // 2, CH)
                group_sum(v + 1 if prep else v)

            group_sum(1)
            for j in pairs(pe, N):
                body(2 * j, 0, j * 4 + 2)
                body(2 * j + 1, 1, j * 4 + 4)
            body(N - 2, 0, 2 * N - 2)
            body(N - 1, 1, 2 * N, prep=False)


def stage2(nc, a, N):
    ctx = ExitStack()
    with ctx:
        def sb(name, shape, dt=F32):
            return ctx.enter_context(nc.sbuf_tensor(name, shape, dt))

        def sem(name):
            return ctx.enter_context(nc.semaphore(name))

        def ps(name, shape):
            return ctx.enter_context(nc.psum_tensor(name, shape, F32))

        xin = [sb(f"xin{b}", [P, 16 * HW]) for b in range(2)]
        xn = sb("xn2", [P, 2, 64 * HW], F16)
        ux = [sb(f"ux{b}", [P, 2, 2, 512], F16) for b in range(2)]
        f32 = sb("f32", [P, 2, 512])
        fx = [sb(f"fx{b}", [P, 2, 2, 512], F16) for b in range(2)]
        y = sb("y", [P, 16, 2, HALF], F16)
        ct = [sb(f"ct{b}", [P, 2, Y1W], F16) for b in range(2)]
        st = [sb(f"sh{b}", [P, 2, Y2W], F16) for b in range(2)]
        cw = [sb(f"cw{b}", [P, 2, 2, 4, 128], F16) for b in range(2)]
        g = sb("g", [P, GN_])
        gp = [sb(f"gp{t}", [P, GW]) for t in range(2)]
        gs = sb("gs", [P, 2, 2, GW], F16)
        gt = [sb(f"gt{k}", [P, 2, 32 * TP], F16) for k in range(KC)]
        yt = [sb(f"yt{k}", [P, 2, HALF], F16) for k in range(KC)]
        res = [sb(f"res{b}", [P, 16, HW]) for b in range(2)]
        co = sb("co2", [P, 2])
        bank = ps("bank", [P, 6, 512])
        pd = ps("pd", [P, 2, 512])

        x_in = [sem("x_in0"), sem("x_in1")]
        co_set = sem("norm2_fetched")
        n32 = sem("normed2_f32")
        nhi = sem("normed2_hi")
        nlo = sem("normed2_lo")
        expand = sem("expand_done")
        uhi = sem("expand_hi")
        ulo = sem("expand_lo")
        fwd = sem("forward_done")
        fm = sem("filtered")
        fhi = sem("filtered_hi")
        flo = sem("filtered_lo")
        inv = sem("inverse_done")
        yhi = sem("y_hi")
        ylo = sem("y_lo")
        y_out = sem("y_stored")
        zpad = sem("pads_zeroed")
        c_in = [sem("group_in0"), sem("group_in1")]
        c3 = sem("dw3_done")
        c5 = sem("dw5_done")
        x1 = sem("x1_summed")
        gl = sem("gelu_done")
        gate = [sem("gate3_done"), sem("gate5_done")]
        ghi = [sem("gate3_hi"), sem("gate5_hi")]
        glo = [sem("gate3_lo"), sem("gate5_lo")]
        g_out = sem("gates_stored")
        d_in = [sem(f"operands_in{k}") for k in range(KC)]
        d_used = [sem(f"operands_used{k}") for k in range(KC)]
        added = sem("projection_added")
        r_in = [sem("residual_in0"), sem("residual_in1")]
        r_out = [sem("residual_out0"), sem("residual_out1")]
        IM = C * HW * HW

        block = ctx.enter_context(nc.Block())

        def image_rows(ap, n, h, row, rows, step):
            return dram(ap, n * IM + (64 * h + row) * HW, [[HW * HW, C], [step * HW, rows], [1, HW]])

        def held(eng):
            eng.wait_ge(zpad, 4)

        def patches(part, q):
            return view(xn[:], part * 8192 + q * 2048, [[16, 16], [256, 8], [1, 16]])

        def piece(q):
            return xin[q % 2][:].rearrange("p (r k w) -> p r k w", r=16, k=8)

        def slots(eng, run):
            run(0, 0, 0)
            run(1, 0, 1)
            with eng.Fori(1, SLOTS // 2) as j:
                run(2 * j, j, 0)
                run(2 * j + 1, j, 1)
            run(SLOTS, SLOTS // 2, 0)
            run(SLOTS + 1, SLOTS // 2, 1)

        def live(s):
            if not isinstance(s, int):
                return True, True, True
            return s < SLOTS, 1 <= s <= SLOTS, s >= 2

        @block.sync
        def _(sp):
            sp.sem_inc(y_out, OPEN)
            sp.sem_inc(g_out, OPEN)
            sp.wait_ge(zpad, 4)
            with sp.Fori(0, N) as n:
                for q in range(4):
                    sp.wait_ge(nlo, n * 4 + q - 1 + CREDIT)
                    for h in range(2):
                        sp.dma_start(view(xin[q % 2][:], 0, [[HW, 16], [1, HW]], C, C * h),
                                     image_rows(a["xs"], n, h, 16 * q, 16, 1)).then_inc(x_in[q % 2], 16)
                with sp.Fori(0, KC) as k:
                    m = n * KC + k
                    sp.wait_ge(ylo, OPEN + m * 2 * SLOTS + 2 * SLOTS)
                    for h in range(2):
                        sp.dma_start(dram(a["Y1"], k * C * 32 * Y1W + 1 + (16 * h + 1) * TP, [[32 * Y1W, C], [Y1W, 32], [1, HALF]]),
                                     view(y[:], 0, [[HALF, 32], [1, HALF]], C, C * h)).then_inc(y_out, 16)
                    for h in range(2):
                        for cl in range(4):
                            sp.dma_start(dram(a["Y2"], k * C * 32 * Y2W + cl * 8 * Y2W + (16 * h + cl // 2) * TP + cl % 2,
                                              [[32 * Y2W, C], [Y2W, 8], [1, HALF]]),
                                         view(y[:], cl * 8 * HALF, [[HALF, 8], [1, HALF]], C, C * h)).then_inc(y_out, 16)
                    def load(j, p):
                        G, gi = m * 8 + j * 2 + p, k * 8 + j * 2 + p
                        sp.wait_ge(c5, G - 1 + CREDIT)
                        sp.wait_ge(x1, G - 1 + CREDIT)
                        sp.dma_start(ct[p][:], dram(a["Y1"], gi * P * 2 * Y1W, [[2 * Y1W, P], [Y1W, 2], [1, Y1W]])).then_inc(c_in[p], 16)
                        sp.dma_start(cw[p][:], dram(a["Cw"], gi * P * 2048, [[2048, P], [1, 2048]])).then_inc(c_in[p], 16)
                        sp.dma_start(st[p][:], dram(a["Y2"], gi * P * 2 * Y2W, [[2 * Y2W, P], [Y2W, 2], [1, Y2W]])).then_inc(c_in[p], 16)

                    def store(j, p):
                        sp.wait_ge(glo[1], OPEN + m * 8 + j * 2 + p + 1)
                        sp.dma_start(dram(a["Gd"], k * P * 32 * GW + (j * 2 + p) * 8 * 32 * GW,
                                          [[2 * GW, P], [C * 32 * GW, 2], [1, 2 * GW]]),
                                     view(gs[:], 0, [[2 * GW, 2], [1, 2 * GW]])).then_inc(g_out, 16)

                    sp.wait_ge(y_out, OPEN + m * 160 + 160)
                    load(0, 0)
                    load(0, 1)
                    with sp.Fori(1, 4) as j:
                        for p in range(2):
                            load(j, p)
                            store(j - 1, p)
                    store(3, 0)
                    store(3, 1)
                with sp.Fori(0, 2) as ih:
                    for il in range(2):
                        for j in range(4):
                            it = n * 16 + ih * 8 + il * 4 + j
                            ij = ih * 8 + (j // 2) * 4 + il * 2 + j % 2
                            if il == 0 and j == 0:
                                sp.wait_ge(g_out, OPEN + n * 16 * NG + 16 * NG)
                            for k in range(KC):
                                sp.wait_ge(d_used[k], OPEN + it)
                                sp.dma_start(gt[k][:], dram(a["Gd"], k * P * 32 * GW + ij * 2 * GW + ih * TP + j // 2,
                                                            [[32 * GW, P], [GW, 2], [1, 32 * TP]])).then_inc(d_in[k], 16)
                                for h in range(2):
                                    sp.dma_start(view(yt[k][:], 0, [[HALF, 2], [1, HALF]], C, C * h),
                                                 dram(a["Y1"], k * C * 32 * Y1W + ij * 2 * Y1W + 1 + (16 * h + 1) * TP,
                                                      [[32 * Y1W, C], [Y1W, 2], [1, HALF]])).then_inc(d_in[k], 16)
            for b in range(2):
                sp.wait_ge(r_out[b], OPEN + 32 * 2 * N)

        @block.gpsimd
        def _(pool):
            pool.sem_inc(glo[0], OPEN)
            pool.sem_inc(glo[1], OPEN)
            pool.sem_inc(flo, OPEN)
            nc.gpsimd.memset(y[:], 0.0).then_inc(zpad, 1)
            nc.gpsimd.memset(gs[:], 0.0).then_inc(zpad, 1)
            nc.gpsimd.memset(gp[0][:], 0.0).then_inc(zpad, 1)
            nc.gpsimd.memset(gp[1][:], 0.0).then_inc(zpad, 1)
            pool.sem_inc(nlo, CREDIT)
            pool.sem_inc(x1, CREDIT)
            with pool.Fori(0, N) as n:
                for q in range(4):
                    pool.wait_ge(nhi, n * 4 + q + 1)
                    nc.gpsimd.tensor_tensor(patches(1, q), piece(q), patches(0, q), ALU.subtract).then_inc(nlo, 1)
                with pool.Fori(0, KC) as k:
                    m = n * KC + k
                    with pool.Fori(0, SLOTS // 2) as j:
                        for p in range(2):
                            pool.wait_ge(fhi, m * SLOTS + j * 2 + p + 1)
                            nc.gpsimd.tensor_tensor(fx[p][:, 1], f32[:], fx[p][:, 0], ALU.subtract).then_inc(flo, 1)
                    with pool.Fori(0, 4) as j:
                        for p in range(2):
                            G = m * 8 + j * 2 + p
                            pool.wait_ge(c_in[p], (m * 4 + j) * 48 + 48)
                            pool.wait_ge(gate[1], OPEN + G)
                            nc.gpsimd.tensor_tensor(g[:], st[p][:, 0, 0:GN_], st[p][:, 1, 0:GN_], ALU.add).then_inc(x1, 1)
                            for t in range(2):
                                pool.wait_ge(ghi[t], G + 1)
                                nc.gpsimd.tensor_tensor(gs[:, t, 1], gp[t][:], gs[:, t, 0], ALU.subtract).then_inc(glo[t], 1)

        @block.scalar
        def _(act):
            act.sem_inc(r_out[0], OPEN)
            act.sem_inc(r_out[1], OPEN)
            act.wait_ge(zpad, 4)
            with act.Fori(0, N) as n:
                nc.scalar.activation(co[:], view(a["norm2"][:], n * 2, [[1, 2]]), ACT.Copy).then_inc(co_set, 1)
                act.wait_ge(co_set, n + 1)
                for q in range(4):
                    act.wait_ge(x_in[q % 2], (n * 2 + q // 2) * 32 + 32)
                    nc.scalar.activation(xin[q % 2][:], xin[q % 2][:], ACT.Identity,
                                         bias=co[:, 1:2], scale=co[:, 0:1]).then_inc(n32, 1)
                    act.wait_ge(n32, n * 4 + q + 1)
                    nc.scalar.activation(patches(0, q), piece(q), ACT.Copy).then_inc(nhi, 1)
                with act.Fori(0, KC) as k:
                    m = n * KC + k
                    act.wait_ge(y_out, OPEN + m * 160)

                    def run(s, j, q):
                        ex, fo, iv = live(s)
                        if ex:
                            act.wait_ge(expand, m * SLOTS + s + 1)
                            act.wait_ge(fwd, m * SLOTS + s - 1 + CREDIT)
                            nc.scalar.activation(ux[q][:, 0], bank[:, 0:2, :], ACT.Copy).then_inc(uhi, 1)
                        if fo:
                            act.wait_ge(fm, OPEN + m * SLOTS + s)
                            act.wait_ge(inv, m * SLOTS + s - 2 + CREDIT)
                            nc.scalar.activation(fx[1 - q][:, 0], f32[:], ACT.Copy).then_inc(fhi, 1)
                        if iv:
                            act.wait_ge(inv, m * SLOTS + s - 1 + CREDIT)
                            held(act)
                            for pw in range(2):
                                nc.scalar.activation(
                                    view(y[:], (j - 1) * 4 * TP + q * 16 + pw * 8, [[2 * HALF, 16], [TP, 4], [1, 8]]),
                                    bank[:, 4 + pw, :].rearrange("p (x a b) -> p x a b", x=16, a=4),
                                    ACT.Copy).then_inc(yhi, 1)

                    slots(act, run)
                    with act.Fori(0, 8) as gi:
                        G = m * 8 + gi
                        act.wait_ge(x1, G + 1 + CREDIT)
                        held(act)
                        nc.scalar.activation(g[:], g[:], ACT.Gelu, scale=view(a["w1g"][:], k * 8 + gi, [[1, 1]])).then_inc(gl, 1)
                        act.wait_ge(g_out, OPEN + G * 16)
                        for t in range(2):
                            act.wait_ge(gate[t], OPEN + G + 1)
                            nc.scalar.activation(gs[:, t, 0], gp[t][:], ACT.Copy).then_inc(ghi[t], 1)
                with act.Fori(0, 2) as ih:
                    for il in range(2):
                        act.wait_ge(r_out[il], OPEN + (n * 2 + ih) * 32)
                        for h in range(2):
                            act.dma_start(view(res[il][:], 0, [[HW, 16], [1, HW]], C, C * h),
                                          image_rows(a["xs"], n, h, ih * 2 + il, 16, 4)).then_inc(r_in[il], 16)
                    for il in range(2):
                        act.wait_ge(added, n * 16 + ih * 8 + il * 4 + 4 + CREDIT)
                        for h in range(2):
                            act.dma_start(image_rows(a["out"], n, h, ih * 2 + il, 16, 4),
                                          view(res[il][:], 0, [[HW, 16], [1, HW]], C, C * h)).then_inc(r_out[il], 16)

        @block.vector
        def _(dve):
            dve.sem_inc(gate[0], OPEN)
            dve.sem_inc(gate[1], OPEN)
            dve.sem_inc(ulo, OPEN)
            dve.sem_inc(fm, OPEN)
            dve.sem_inc(ylo, OPEN)
            dve.sem_inc(added, CREDIT)
            dve.wait_ge(zpad, 4)
            with dve.Fori(0, N) as n:
                with dve.Fori(0, KC) as k:
                    m = n * KC + k

                    def run(s, j, q):
                        ex, fo, iv = live(s)
                        if ex:
                            dve.wait_ge(uhi, m * SLOTS + s + 1)
                            nc.vector.tensor_tensor(ux[q][:, 1], bank[:, 0:2, :], ux[q][:, 0], ALU.subtract).then_inc(ulo, 1)
                        if fo:
                            dve.wait_ge(fwd, m * SLOTS + s + CREDIT)
                            dve.wait_ge(flo, OPEN + m * SLOTS + s - 1)
                            for mh in range(2):
                                last = nc.vector.tensor_tensor(
                                    f32[:, mh, :].rearrange("p (a c) -> p a c", c=C),
                                    bank[:, 2 + mh, :].rearrange("p (a c) -> p a c", c=C),
                                    view(a["wf"][:], mh * HID + k * C, [[0, 8], [1, C]]), ALU.mult)
                            last.then_inc(fm, 1)
                        if iv:
                            for pw in range(2):
                                dve.wait_ge(yhi, (m * SLOTS + s - 2) * 2 + pw + 1)
                                dst = view(y[:], (j - 1) * 4 * TP + q * 16 + pw * 8, [[2 * HALF, 16], [TP, 4], [1, 8]])
                                lo = view(y[:], HALF + (j - 1) * 4 * TP + q * 16 + pw * 8, [[2 * HALF, 16], [TP, 4], [1, 8]])
                                nc.vector.tensor_tensor(lo, bank[:, 4 + pw, :].rearrange("p (x a b) -> p x a b", x=16, a=4), dst,
                                                        ALU.subtract).then_inc(ylo, 1)

                    slots(dve, run)
                    with dve.Fori(0, 8) as gi:
                        G = m * 8 + gi
                        dve.wait_ge(gl, G + 1)
                        for t, done in ((0, c3), (1, c5)):
                            dve.wait_ge(done, G + 1 + (CREDIT if t else 0))
                            dve.wait_ge(glo[t], OPEN + G)
                            nc.vector.tensor_tensor(gp[t][:, 0:GN_].rearrange("p (b n) -> p b n", b=3),
                                                    bank[:, 3 * t:3 * t + 3, 0:NB],
                                                    g[:].rearrange("p (b n) -> p b n", b=3), ALU.mult).then_inc(gate[t], 1)
                with dve.Fori(0, 2) as ih:
                    for il in range(2):
                        dve.wait_ge(r_in[il], (n * 2 + ih) * 32 + 32)
                        for j in range(4):
                            dve.wait_ge(d_used[KC - 1], OPEN + n * 16 + ih * 8 + il * 4 + j + 1)
                            rows = view(res[il][:], j, [[HW, 16], [4, 32]])
                            nc.vector.tensor_tensor(rows, pd[:, j % 2, :].rearrange("p (a b) -> p a b", b=32), rows,
                                                    ALU.add).then_inc(added, 1)

        @block.tensor
        def _(pe):
            for k in range(KC):
                pe.sem_inc(d_used[k], OPEN)
            pe.sem_inc(fwd, CREDIT)
            pe.sem_inc(inv, CREDIT)
            pe.sem_inc(c5, CREDIT)
            with pe.Fori(0, N) as n:
                with pe.Fori(0, KC) as k:
                    m = n * KC + k
                    pe.wait_ge(nlo, n * 4 + 4 + CREDIT)
                    pe.wait_ge(gate[1], OPEN + m * 8)

                    def run(s, j, q):
                        ex, fo, iv = live(s)
                        if ex:
                            pe.wait_ge(ulo, OPEN + m * SLOTS + s)
                            for r in range(2):
                                for pw in range(4):
                                    for t, (wi, di) in enumerate(SPLITS):
                                        last = nc.tensor.matmul(
                                            bank[:, r, pw * 128:(pw + 1) * 128],
                                            view(xn[:], di * 8192 + ((j * 8 + q * 4 + pw) * 2 + r) * 128, [[1, 128]]),
                                            view(a["Win"][:], (wi * KC + k) * 128, [[1, 128]]), start=(t == 0), stop=(t == 2))
                            last.then_inc(expand, 1)
                        if fo:
                            pe.wait_ge(ulo, OPEN + m * SLOTS + s)
                            pe.wait_ge(fm, OPEN + m * SLOTS + s - 1)
                            for mh in range(2):
                                t = 0
                                for r in range(2):
                                    for wi, di in SPLITS:
                                        last = nc.tensor.matmul(bank[:, 2 + mh, :], a["Bf"][:, wi, r, mh, :],
                                                                ux[1 - q][:, di, r, :], start=(t == 0), stop=(t == 5))
                                        t += 1
                            last.then_inc(fwd, 1)
                        if iv:
                            pe.wait_ge(flo, OPEN + m * SLOTS + s - 1)
                            pe.wait_ge(ylo, OPEN + (m * SLOTS + s - 2) * 2)
                            for pw in range(4):
                                t = 0
                                for mh in range(2):
                                    for wi, di in SPLITS:
                                        last = nc.tensor.matmul(
                                            view(bank[:], (4 + pw // 2) * 512 + (pw % 2) * 4, [[8, 64], [1, 4]]),
                                            fx[q][:, di, mh, pw * 128:(pw + 1) * 128], a["Bi"][:, wi, mh, :],
                                            start=(t == 0 and pw % 2 == 0), stop=(t == 5), skip_group_check=True)
                                        t += 1
                            last.then_inc(inv, 1)

                    slots(pe, run)
                    with pe.Fori(0, 4) as j:
                        for p in range(2):
                            G = m * 8 + j * 2 + p
                            pe.wait_ge(c_in[p], (m * 4 + j) * 48 + 48)
                            pe.wait_ge(ylo, OPEN + (m + 1) * SLOTS * 2)
                            for x, done in ((0, c3), (1, c5)):
                                pe.wait_ge(gate[x], OPEN + G)
                                t = 0
                                for q in range(4):
                                    for wi, di in SPLITS:
                                        for b in range(3):
                                            last = nc.tensor.matmul(
                                                bank[:, 3 * x + b, 0:NB], cw[p][:, wi, x, q, :],
                                                view(ct[p][:], di * Y1W + b * NB + (q // 2) * TP + q % 2, [[1, NB]]),
                                                start=(t == 0), stop=(t == 11))
                                        t += 1
                                last.then_inc(done, 1)
                with pe.Fori(0, 2) as ih:
                    for il in range(2):
                        for j in range(4):
                            it = n * 16 + ih * 8 + il * 4 + j
                            pe.wait_ge(added, it - 1 + CREDIT)
                            for k in range(KC):
                                pe.wait_ge(d_in[k], it * 48 + 48)
                                for wi, di in SPLITS:
                                    nc.tensor.matmul(pd[:, j % 2, :], a["W3"][:, wi, k, :],
                                                     view(yt[k][:], di * HALF, [[TP, 16], [1, 32]]),
                                                     start=(k == 0 and wi + di == 0), stop=False, skip_group_check=True)
                                for wi, di in SPLITS:
                                    for h in range(2):
                                        last = nc.tensor.matmul(
                                            pd[C * h:C * h + C, j % 2, :], a["Wg"][:, wi, k, :],
                                            view(gt[k][:], (di * 32 + 16 * h) * TP, [[TP, 16], [1, 32]]),
                                            start=False, stop=(k == KC - 1 and wi == 1), skip_group_check=True)
                                last.then_inc(d_used[k], 1)


def program(nc, a, N):
    ctx = ExitStack()
    with ctx:
        for name, shape, dt in (
            ("Wc", [P, 2, 12, 128], F16),
            ("Win", [P, 2, KC, 128], F16),
            ("W3", [P, 2, KC, 128], F16),
            ("Wg", [P, 2, KC, 64], F16),
            ("Bf", [P, 2, 2, 2, 128], F16),
            ("Bi", [P, 2, 2, 256], F16),
            ("wf", [P, 2, HID], F32),
            ("w1g", [P, NG], F32),
            ("ident", [P, 128], F32),
            ("gmask", [P, 128], F32),
            ("norm2", [P, N, 2], F32),
        ):
            a[name] = ctx.enter_context(nc.sbuf_tensor("c_" + name, shape, dt))
        a["ws"] = nc.dram_tensor("ws", (65536,), F32, kind="Internal").ap()
        a["xs"] = nc.dram_tensor("xs", (N * C * HW * HW,), F32, kind="Internal").ap()
        a["Cw"] = nc.dram_tensor("Cw", (NG * P * 2048,), F16, kind="Internal").ap()
        a["Y1"] = nc.dram_tensor("Y1", (HID * 32 * Y1W,), F16, kind="Internal").ap()
        a["Y2"] = nc.dram_tensor("Y2", (HID * 32 * Y2W,), F16, kind="Internal").ap()
        a["Gd"] = nc.dram_tensor("Gd", (KC * P * 32 * GW,), F16, kind="Internal").ap()
        stage0(nc, a)
        stage1(nc, a, N)
        stage2(nc, a, N)



def _tile_order():
    return [(2 * ih + il, 2 * jh + jl) for ih in range(2) for jh in range(2) for il in range(2) for jl in range(2)]


def _basis():
    r, w = np.meshgrid(np.arange(16), np.arange(16), indexing="ij")
    phi, pos, neg = [], [], []
    for ky in range(9):
        for kx in range(16):
            arg = 2 * np.pi * (kx * r + ky * w) / 16
            if ky in (0, 8):
                if kx > 8:
                    continue
                fs = [np.cos(arg)] if kx in (0, 8) else [np.sqrt(2) * np.cos(arg), np.sqrt(2) * np.sin(arg)]
                other = (16 - kx) % 16
            else:
                fs = [np.sqrt(2) * np.cos(arg), np.sqrt(2) * np.sin(arg)]
                other = kx
            for f in fs:
                phi.append(f / 4)
                pos.append(kx * 9 + ky)
                neg.append(other * 9 + ky)
    return np.array(phi), np.array(pos), np.array(neg)


def _split(v):
    hi = v.astype(np.float16)
    return np.stack([hi, (v - hi.astype(np.float64)).astype(np.float16)])


def _layouts(x, L0_conv_gates, L1_conv_w_in, L1_conv_fft_w, L1_conv_w1, L1_conv_w3, L1_conv_w5, L1_conv_w_out):
    N = x.shape[0]
    perm = np.arange(C).reshape(2, 2, 16).transpose(1, 0, 2).reshape(-1)
    d = {}
    d["x"] = np.ascontiguousarray(x[:, perm]).reshape(-1)
    gates = np.asarray(L0_conv_gates).reshape(3, 15, 4, 4)
    row = np.arange(256).reshape(2, P)
    pair = np.stack([(row >> s) & 3 for s in (6, 4, 2, 0)])
    gi = np.arange(4)[:, None, None]
    d["ge"] = np.stack([gates[:, gi + 4 * op, pair] for op in range(2)], 1).transpose(4, 0, 1, 3, 2, 5)
    p = np.arange(P)
    mid = np.stack([(p >> s) & 3 for s in (5, 3, 1)])
    g3 = np.arange(3)[:, None]
    d["go"] = np.concatenate([gates[:, 8 + g3, mid], gates[:, 12 + g3, mid]], 1).transpose(2, 0, 1, 3)
    cross = gates[:, 11].reshape(3, 2, 2, 2, 2)[:, p & 1]
    d["gx"] = cross.transpose(1, 0, 2, 4, 3)
    d["i2"] = (p[:, None] & 1 == np.arange(2)).astype(np.float32)
    d["d_ident"] = np.eye(P, dtype=np.float32)
    grp = (p % C) // 2
    d["d_gmask"] = (grp[:, None] == grp[None]).astype(np.float32) / 4
    d["cmask"] = (p[:, None] // 16 == np.arange(8)).astype(np.float32)
    order = _tile_order()
    oi = np.array([o[0] for o in order])
    oj = np.array([o[1] for o in order])
    q = np.arange(4)
    dh = 4 * (q // 2)[None, :, None] + oi[:, None, None] - ((oi + 2) % 4)[None, None, :]
    dw = 4 * (q % 2)[None, :, None] + oj[:, None, None] - ((oj + 2) % 4)[None, None, :]
    def taps(w, size, shift):
        w = np.pad(np.asarray(w).reshape(HID, size, size), ((0, 0), (4, 4), (4, 4)))
        return w[:, dh - shift + 4, dw - shift + 4]
    tab = np.stack([taps(L1_conv_w3, 3, 1), taps(L1_conv_w5, 5, 0)], 2)
    d["tab"] = tab.reshape(NG, P, 128).transpose(1, 0, 2)
    w1 = np.asarray(L1_conv_w1).reshape(HID)
    d["w1c"] = w1.reshape(KC, C)[:, p % C].T
    d["d_w1g"] = w1.reshape(NG, 8)[:, p // 16].T
    d["win"] = np.asarray(L1_conv_w_in).reshape(HID, C)[:, perm].T.reshape(-1)
    d["wout"] = np.asarray(L1_conv_w_out).reshape(C, 3 * HID)[perm].T.reshape(-1)
    phi, pos, neg = _basis()
    fw = np.asarray(L1_conv_fft_w).reshape(HID, 144)
    d["fw"] = np.stack([fw[:, pos], fw[:, neg]]).reshape(2, HID, 2, P).transpose(3, 2, 0, 1)
    d["d_Bf"] = _split(phi.reshape(2, P, 2, 8, 16).transpose(3, 4, 2, 0, 1).reshape(P, 2, 2, P)).transpose(1, 0, 2, 3, 4)
    tiles = phi.reshape(256, 4, 4, 4, 4)[:, :, oi, :, :]
    tiles = tiles[:, :, np.arange(16), :, oj]
    d["d_Bi"] = _split(tiles.transpose(1, 0, 2, 3).reshape(2, P, 256).transpose(1, 0, 2)).transpose(1, 0, 2, 3)
    return {k: np.ascontiguousarray(v) for k, v in d.items()}, perm, N


def kernel(x, L0_conv_gates, L1_conv_w_in, L1_conv_fft_w, L1_conv_w1, L1_conv_w3, L1_conv_w5, L1_conv_w_out):
    import concourse.bacc as bacc
    from concourse.bass_utils import run_bass_kernel_spmd

    arrays, perm, N = _layouts(x, L0_conv_gates, L1_conv_w_in, L1_conv_fft_w, L1_conv_w1, L1_conv_w3, L1_conv_w5, L1_conv_w_out)
    nc = bacc.Bacc("TRN2", target_bir_lowering=False, num_devices=1)
    a = {k: nc.dram_tensor("in_" + k, v.shape, mybir.dt.from_np(v.dtype), kind="ExternalInput").ap() for k, v in arrays.items()}
    a["out"] = nc.dram_tensor("out_dram", (N * C * HW * HW,), F32, kind="ExternalOutput").ap()
    program(nc, a, N)
    r = run_bass_kernel_spmd(nc, [{"in_" + k: v for k, v in arrays.items()}], core_ids=[0])
    out = r.results[0]["out_dram"].reshape(N, C, HW, HW)
    return out[:, np.argsort(perm)]
```

```python
from contextlib import ExitStack

import concourse.bass as bass
import numpy as np
from concourse import mybir

F32 = mybir.dt.float32
F16 = mybir.dt.float16
ALU = mybir.AluOpType
ACT = mybir.ActivationFunctionType

P = 128
C = 64
HW = 128
RP = HW // 2
HID = 192
KC = HID // C
EPS = 1e-5
FR_W = 132
XS_W = 130
CH = 16
TP = 33
HALF = 16 * TP
Y1W = 1124
GN_ = 33 * TP
GW = 1090
NB = GN_ // 3
NG = HID // 8
SLOTS = 8
OPEN = 1
CREDIT = 2
Y1N = HID * 32 * Y1W
GDN = KC * P * 32 * GW
SPLITS = ((0, 0), (0, 1), (1, 0))


def view(ap, off, dims, parts=None, p0=0):
    step = ap.ap[0][0]
    n = ap.ap[0][1] if parts is None else parts
    return bass.AP(tensor=ap.tensor, offset=ap.offset + p0 * step + off, ap=[[step, n]] + [list(d) for d in dims])


def dram(ap, off, dims):
    return bass.AP(tensor=ap.tensor, offset=ap.offset + off, ap=[list(d) for d in dims])


def pairs(eng, N):
    if N > 2:
        with eng.Fori(0, N // 2 - 1) as j:
            yield j


def stage0(nc, a):
    ctx = ExitStack()
    with ctx:
        def sb(name, shape, dt=F32):
            return ctx.enter_context(nc.sbuf_tensor(name, shape, dt))

        def sem(name):
            return ctx.enter_context(nc.semaphore(name))

        ge = sb("ge", [P, 3, 2, 2, 4, 4])
        go = sb("go", [P, 3, 6, 4])
        gx = sb("gx", [P, 3, 4, 2])
        i2 = sb("i2", [P, 2])
        K = sb("K", [P, 2, 2, 256])
        R = sb("R", [P, 4, 128])
        Cm = sb("Cm", [P, 128])
        o16 = sb("o16", [P, 2, 16])
        o64 = sb("o64", [P, 2, 64])
        S = sb("S", [P, 2, 256])
        T = sb("T", [P, 2, 256])
        Wo = sb("Wo", [C, 1024])
        Wt = sb("Wt", [C, 12, 2, 2, 2, 2, 16])
        tab = sb("tab", [P, NG, 128])
        zero = sb("zero", [P, 96 * 36], F16)
        win32 = sb("win32", [P, KC, 128])
        wout32 = sb("wout32", [P, KC, 128])
        wg32 = sb("wg32", [P, KC, 64])
        w1c = sb("w1c", [P, KC])
        fw = sb("fw", [P, 2, 2, HID])
        psT = ctx.enter_context(nc.psum_tensor("psT", [P, 2, 256], F32))
        psS = ctx.enter_context(nc.psum_tensor("psS", [P, 2, 256], F32))
        psW = ctx.enter_context(nc.psum_tensor("psW", [P, 12, 128], F32))

        gates_in = sem("gates_in")
        consts_in = sem("consts_in")
        blocks_in = sem("blocks_in")
        zeroed = sem("zeroed")
        step = sem("dve_step")
        mats = sem("mats_built")
        pe_step = sem("pe_step")
        ev = sem("state_evacuated")
        s_out = sem("state_stored")
        s_in = sem("weight_loaded")
        wt_done = sem("taps_laid_out")
        wtr = sem("taps_transposed")
        whi = sem("conv_weight_hi")
        zst = sem("frames_zeroed")
        cst = sem("const_hi")
        n_gates, n_consts, n_blocks = 4, 11, 8

        block = ctx.enter_context(nc.Block())

        @block.sync
        def _(sp):
            sp.dma_start(ge[:], a["ge"]).then_inc(gates_in, 16)
            sp.dma_start(go[:], a["go"]).then_inc(gates_in, 16)
            sp.dma_start(gx[:], a["gx"]).then_inc(gates_in, 16)
            sp.dma_start(i2[:], a["i2"]).then_inc(gates_in, 16)
            sp.dma_start(a["ident"][:], a["d_ident"]).then_inc(consts_in, 16)
            sp.dma_start(a["gmask"][:], a["d_gmask"]).then_inc(consts_in, 16)
            sp.dma_start(tab[:], a["tab"]).then_inc(consts_in, 16)
            sp.dma_start(a["cmask"][:], a["d_cmask"]).then_inc(consts_in, 16)
            sp.dma_start(a["Bf"][:], a["d_Bf"]).then_inc(consts_in, 16)
            sp.dma_start(a["Bi"][:], a["d_Bi"]).then_inc(consts_in, 16)
            sp.dma_start(fw[:], a["fw"]).then_inc(consts_in, 16)
            sp.dma_start(a["w1g"][:], a["d_w1g"]).then_inc(consts_in, 16)
            sp.dma_start(w1c[:], a["w1c"]).then_inc(consts_in, 16)
            for t in range(2):
                sp.dma_start(view(wg32[:], 0, [[64, KC], [1, 64]], C, C * t),
                             dram(a["wout"], t * HID * C, [[C, C], [C * C, KC], [1, C]])).then_inc(consts_in, 16)
            sp.wait_ge(zeroed, 2)
            for h in range(2):
                for k in range(KC):
                    sp.dma_start(view(win32[:], k * 128 + C * h, [[1, C]], C, C * h),
                                 dram(a["win"], k * C, [[HID, C], [1, C]])).then_inc(blocks_in, 16)
                sp.dma_start(view(wout32[:], C * h, [[128, KC], [1, 64]], C, C * h),
                             dram(a["wout"], 2 * HID * C, [[C, C], [C * C, KC], [1, C]])).then_inc(blocks_in, 16)
            sp.wait_ge(zeroed, 3)
            rows = HID * 32 // 64
            for par in range(2):
                for off in (0, Y1W - 34):
                    sp.dma_start(dram(a["Y1"], par * Y1N + off, [[Y1W * rows, 64], [Y1W, rows], [1, 34]]),
                                 view(zero[:], 0, [[34, rows], [1, 34]], 64)).then_inc(zst, 16)
            sp.wait_ge(ev, 13)
            sp.dma_start(dram(a["ws"], 0, [[256, P], [P * 256, 2], [1, 256]]), S[:]).then_inc(s_out, 16)
            sp.wait_ge(s_out, 16)
            for u in range(2):
                for t in range(2):
                    sp.dma_start(view(Wo[:], 0, [[1, 1024]], 16, 32 * u + 16 * t),
                                 dram(a["ws"], (32 * t + 16 * u) * 1024, [[1024, 16], [1, 1024]])).then_inc(s_in, 16)
            sp.wait_ge(zst, 64)

        @block.gpsimd
        def _(pool):
            nc.gpsimd.memset(win32[:], 0.0).then_inc(zeroed, 1)
            nc.gpsimd.memset(wout32[:], 0.0).then_inc(zeroed, 1)
            nc.gpsimd.memset(zero[:], 0.0).then_inc(zeroed, 1)

        @block.vector
        def _(dve):
            n = [0]

            def link(ins):
                n[0] += 1
                ins.then_inc(step, 1)
                dve.wait_ge(step, n[0])

            def outer(out, off, x, xoff, y, yoff, nx, ny, outs=None):
                so, sx, sy, b = outs or (0, 0, 0, 1)
                return nc.vector.tensor_tensor(view(out[:], off, [[so, b], [ny, nx], [1, ny]]),
                                               view(x[:], xoff, [[sx, b], [1, nx], [0, ny]]),
                                               view(y[:], yoff, [[sy, b], [0, nx], [1, ny]]), ALU.mult)

            link(nc.vector.memset(S[:], 0.0))
            nc.vector.memset(S[0:1, 0, 0:1], 1.0).then_inc(ev, 1)
            link(nc.vector.memset(Wt[:], 0.0))
            dve.wait_ge(gates_in, 16 * n_gates)
            for r in range(3):
                if r:
                    dve.wait_ge(pe_step, 4 * r)
                for op in range(2):
                    g0 = (r * 2 + op) * 32
                    link(outer(o16, 0, ge, g0, ge, g0 + 4, 4, 4, (16, 16, 16, 2)))
                    link(outer(o64, 0, o16, 0, ge, g0 + 8, 16, 4, (64, 16, 16, 2)))
                    outer(K, op * 512, o64, 0, ge, g0 + 12, 64, 4, (256, 64, 16, 2)).then_inc(mats, 1)
                    dve.wait_ge(mats, 4 * r + op + 1)
                g0 = r * 24
                link(outer(o16, 0, go, g0, go, g0 + 4, 4, 4))
                link(outer(o64, 0, o16, 0, go, g0 + 8, 16, 4))
                outer(R, 0, o64, 0, gx, r * 8, 64, 2, (128, 0, 2, 4)).then_inc(mats, 1)
                dve.wait_ge(mats, 4 * r + 3)
                link(outer(o16, 0, go, g0 + 12, go, g0 + 16, 4, 4))
                link(outer(o64, 0, o16, 0, go, g0 + 20, 16, 4))
                outer(Cm, 0, o64, 0, i2, 0, 64, 2).then_inc(mats, 1)
                for q, (dst, src) in enumerate(((T, psT), (S, psS), (T, psT), (S, psS))):
                    dve.wait_ge(pe_step, 4 * r + q + 1)
                    if q == 3 and r < 2:
                        nc.vector.tensor_scalar(dst[:], src[:], 0.0, None, ALU.max).then_inc(ev, 1)
                    else:
                        nc.vector.tensor_copy(dst[:], src[:]).then_inc(ev, 1)
            dve.wait_ge(consts_in, 16 * n_consts)
            dve.wait_ge(blocks_in, 16 * n_blocks)
            link(nc.vector.tensor_tensor(fw[:, :, 0, :], fw[:, :, 0, :], fw[:, :, 1, :], ALU.add))
            nc.vector.tensor_scalar(a["wf"][:], fw[:, :, 0, :], 0.5 / 16, None, ALU.mult).then_inc(cst, 1)
            for k in range(KC):
                link(nc.vector.tensor_scalar(wout32[:, k, :], wout32[:, k, :], w1c[:, k:k + 1], None, ALU.mult))
            for t32, hl in ((win32, a["Win"]), (wout32, a["W3"]), (wg32, a["Wg"])):
                link(nc.vector.tensor_copy(hl[:, 0], t32[:]))
                nc.vector.tensor_tensor(hl[:, 1], t32[:], hl[:, 0], ALU.subtract).then_inc(cst, 1)
            for part in range(2):
                for at, g0, g1 in ((0, 0, NG), (NG, 0, 1)):
                    dst = view(a["tabs"][:], at * 256 + part * 128, [[256, g1 - g0], [1, 128]])
                    if part == 0:
                        link(nc.vector.tensor_copy(dst, tab[:, g0:g1, :]))
                    else:
                        nc.vector.tensor_tensor(dst, tab[:, g0:g1, :], view(a["tabs"][:], at * 256, [[256, g1 - g0], [1, 128]]),
                                                ALU.subtract).then_inc(cst, 1)
            dve.wait_ge(s_in, 64)
            for si in range(3):
                for po in range(2):
                    for pi in range(2):
                        for t in range(2):
                            kh = 2 * (si - 1) + pi - po + 2 - t
                            if 0 <= kh < 4:
                                last = nc.vector.tensor_copy(
                                    view(Wt[:], si * 1024 + po * 128 + pi * 64 + t * 16, [[256, 4], [32, 2], [1, 16]]),
                                    view(Wo[:], t * 32 * 16 + kh * 4, [[1, 4], [256, 2], [16, 16]]))
            last.then_inc(wt_done, 1)
            dve.wait_ge(whi, 1)
            nc.vector.tensor_tensor(a["Wc"][:, 1], psW[:], a["Wc"][:, 0], ALU.subtract).then_inc(cst, 1)

        @block.scalar
        def _(act):
            act.wait_ge(wtr, 1)
            nc.scalar.activation(a["Wc"][:, 0], psW[:], ACT.Copy).then_inc(whi, 1)

        @block.tensor
        def _(pe):
            for r in range(3):
                for q in range(4):
                    pe.wait_ge(ev, 4 * r + q + 1)
                    pe.wait_ge(mats, 4 * r + q + 1)
                    if q < 2:
                        src, dst = (S, psT) if q == 0 else (T, psS)
                        for m in range(2):
                            for kb in range(2):
                                last = nc.tensor.matmul(dst[:, m, :], src[:, kb, m * 128:(m + 1) * 128], K[:, q, kb, :],
                                                        start=(kb == 0), stop=(kb == 1))
                    elif q == 2:
                        for bo in range(2):
                            for kb in range(2):
                                for b in range(2):
                                    last = nc.tensor.matmul(psT[:, bo, kb * 128:(kb + 1) * 128],
                                                            S[:, kb, b * 128:(b + 1) * 128], R[:, 2 * b + bo, :],
                                                            start=(b == 0), stop=(b == 1))
                    else:
                        for m in range(2):
                            for cb in range(2):
                                last = nc.tensor.matmul(psS[:, m, cb * 128:(cb + 1) * 128],
                                                        T[:, cb, m * 128:(m + 1) * 128], Cm[:], start=True, stop=True)
                    last.then_inc(pe_step, 1)
            pe.wait_ge(wt_done, 1)
            pe.wait_ge(consts_in, 16 * n_consts)
            for tk in range(12):
                for po in range(2):
                    last = nc.tensor.matmul(psW[:, tk, po * C:(po + 1) * C],
                                            view(Wt[:], tk * 256 + po * 128, [[1, 128]]),
                                            a["ident"][0:C, 0:C], start=True, stop=True, is_transpose=True)
            last.then_inc(wtr, 1)


def stage1(nc, a, N):
    ctx = ExitStack()
    with ctx:
        def sb(name, shape, dt=F32):
            return ctx.enter_context(nc.sbuf_tensor(name, shape, dt))

        def sem(name):
            return ctx.enter_context(nc.semaphore(name))

        raw = sb("raw", [P, RP, XS_W])
        img = [sb(f"img{b}", [P, RP, HW]) for b in range(2)]
        xn = [sb(f"xn{b}", [P, 2, RP + 2, FR_W], F16) for b in range(2)]
        st1 = sb("st1", [P, CH, 6])
        st2 = sb("st2", [P, CH, 6])
        mv = sb("mv", [P, 2])
        tmp = sb("tmp", [P, 4])
        sd = sb("sd", [P, 1])
        co = sb("co", [P, 2])
        zcol = sb("zcol", [P, 16, 1])
        psC = ctx.enter_context(nc.psum_tensor("psC", [P, 2, 512], F32))
        psG = ctx.enter_context(nc.psum_tensor("psG", [P, 2], F32))

        img_in = [sem("img_in0"), sem("img_in1")]
        raw_in = sem("raw_in")
        img_out = [sem("img_out0"), sem("img_out1")]
        pads = sem("frames_cleared")
        step = sem("dve_step1")
        mom = sem("moments_ready")
        gsum = sem("group_sums")
        vready = sem("variance_ready")
        root = sem("root_ready")
        coef = sem("norm_coef")
        n32 = sem("normed_f32")
        nhi = sem("normed_hi")
        lows = sem("low_halves")
        nlo = sem("normed_lo")
        taken = sem("stats_taken")
        conv = sem("conv_done")
        added = sem("residual_added")

        block = ctx.enter_context(nc.Block())
        xi, xs = a["x"], a["xs"]
        IM = C * HW * HW

        def load_img(eng, n, b):
            for par in range(2):
                eng.dma_start(view(img[b][:], 0, [[HW, RP], [1, HW]], C, C * par),
                              dram(xi, n * IM + par * HW, [[HW * HW, C], [2 * HW, RP], [1, HW]])).then_inc(img_in[b], 16)

        def load_raw(eng, n):
            for par in range(2):
                for u in range(2):
                    eng.dma_start(view(raw[:], 1 - u, [[XS_W, RP], [1, HW]], 32, C * par + 32 * u),
                                  dram(xi, n * IM + u * 32 * HW * HW + par * HW,
                                       [[HW * HW, 32], [2 * HW, RP], [1, HW]])).then_inc(raw_in, 16)

        @block.sync
        def _(sp):
            sp.sem_inc(img_out[0], OPEN)
            sp.sem_inc(img_out[1], OPEN)
            def prep(n, b, m):
                sp.wait_ge(img_out[b], OPEN + m * 32)
                if not isinstance(n, int) or n:
                    sp.wait_ge(mom, 2 * n - 1)
                load_img(sp, n, b)
                sp.wait_ge(nlo, OPEN + n * 4)
                load_raw(sp, n)

            def post(n, b):
                sp.wait_ge(added, n * CH + CH + CREDIT)
                for par in range(2):
                    sp.dma_start(dram(xs, n * IM + par * HW, [[HW * HW, C], [2 * HW, RP], [1, HW]]),
                                 view(img[b][:], 0, [[HW, RP], [1, HW]], C, C * par)).then_inc(img_out[b], 16)

            sp.wait_ge(pads, 4)
            prep(0, 0, 0)
            for j in pairs(sp, N):
                prep(2 * j + 1, 1, j)
                post(2 * j, 0)
                prep(2 * j + 2, 0, j + 1)
                post(2 * j + 1, 1)
            prep(N - 1, 1, N // 2 - 1)
            post(N - 2, 0)
            post(N - 1, 1)
            sp.wait_ge(img_out[0], OPEN + 32 * (N // 2))
            sp.wait_ge(img_out[1], OPEN + 32 * (N // 2))

        @block.gpsimd
        def _(pool):
            pool.sem_inc(nlo, OPEN)
            nc.gpsimd.memset(raw[:], 0.0).then_inc(pads, 1)
            nc.gpsimd.memset(xn[0][:], 0.0).then_inc(pads, 1)
            nc.gpsimd.memset(xn[1][:], 0.0).then_inc(pads, 1)
            nc.gpsimd.memset(zcol[:], 0.0).then_inc(pads, 1)
            pool.wait_ge(pads, 4)

            def prep(n, b):
                for q in range(4):
                    pool.wait_ge(nlo, OPEN + n * 4 + q)
                    pool.wait_ge(nhi, n * 4 + q + 1)
                    rows = slice(16 * q, 16 * q + 16)
                    frame = slice(16 * q + 1, 16 * q + 17)
                    nc.gpsimd.tensor_tensor(xn[b][:, 1, frame, 1:130], raw[:, rows, 0:129], xn[b][:, 0, frame, 1:130],
                                            ALU.subtract).then_inc(lows, 1)
                    pool.wait_ge(lows, n * 4 + q + 1)
                    for part in range(4):
                        col = 1 if part % 2 == 0 else 129
                        edge = slice(32 * part, 32 * part + 32)
                        for border in (raw[edge, rows, col - 1:col], xn[b][edge, 0, frame, col:col + 1], xn[b][edge, 1, frame, col:col + 1]):
                            last = nc.gpsimd.tensor_tensor(border, zcol[edge], zcol[edge], ALU.add)
                    last.then_inc(nlo, 1)

            prep(0, 0)
            for j in pairs(pool, N):
                prep(2 * j + 1, 1)
                prep(2 * j + 2, 0)
            prep(N - 1, 1)

        @block.scalar
        def _(act):
            def sqrt_step(v):
                act.wait_ge(vready, v)
                nc.scalar.activation(sd[:], tmp[:, 0:1], ACT.Sqrt).then_inc(root, 1)

            def prep(n, b, v):
                sqrt_step(v)
                act.wait_ge(coef, n + 1)
                act.wait_ge(raw_in, n * 64 + 64)
                if not isinstance(n, int) or n:
                    act.wait_ge(conv, OPEN + (n - 1) * CH)
                for q in range(4):
                    rows = slice(16 * q, 16 * q + 16)
                    nc.scalar.activation(raw[:, rows, 0:129], raw[:, rows, 0:129], ACT.Identity,
                                         bias=co[:, 1:2], scale=co[:, 0:1]).then_inc(n32, 1)
                    act.wait_ge(n32, n * 4 + q + 1)
                    nc.scalar.activation(xn[b][:, 0, 16 * q + 1:16 * q + 17, 1:130], raw[:, rows, 0:129],
                                         ACT.Copy).then_inc(nhi, 1)

            prep(0, 0, 1)
            for j in pairs(act, N):
                prep(2 * j + 1, 1, j * 4 + 2)
                sqrt_step(j * 4 + 3)
                prep(2 * j + 2, 0, j * 4 + 4)
                sqrt_step(j * 4 + 5)
            prep(N - 1, 1, 2 * N - 2)
            sqrt_step(2 * N - 1)
            sqrt_step(2 * N)

        @block.vector
        def _(dve):
            def link(ins, n):
                ins.then_inc(step, 1)
                dve.wait_ge(step, n)

            LINKS = 9

            def coefs(stats, v, out, done):
                n = (v - 1) * LINKS
                dve.wait_ge(taken, v)
                nc.vector.memset(tmp[:, 3:4], 0.0)
                link(nc.vector.bn_aggr(mv[:], stats[:]), n + 1)
                link(nc.vector.tensor_tensor(tmp[:, 1:2], mv[:, 0:1], mv[:, 0:1], ALU.mult), n + 2)
                nc.vector.tensor_tensor(mv[:, 1:2], mv[:, 1:2], tmp[:, 1:2], ALU.add).then_inc(mom, 1)
                dve.wait_ge(gsum, v)
                link(nc.vector.tensor_copy(mv[:], psG[:]), n + 3)
                link(nc.vector.tensor_tensor(tmp[:, 1:2], mv[:, 0:1], mv[:, 0:1], ALU.mult), n + 4)
                link(nc.vector.tensor_tensor(tmp[:, 0:1], mv[:, 1:2], tmp[:, 1:2], ALU.subtract), n + 5)
                nc.vector.tensor_scalar(tmp[:, 0:1], tmp[:, 0:1], EPS, None, ALU.add).then_inc(vready, 1)
                dve.wait_ge(root, v)
                link(nc.vector.reciprocal(tmp[:, 1:2], sd[:]), n + 6)
                link(nc.vector.scalar_tensor_tensor(tmp[:, 2:3], tmp[:, 1:2], tmp[:, 1:2], tmp[:, 0:1], ALU.mult, ALU.mult), n + 7)
                link(nc.vector.tensor_scalar(tmp[:, 2:3], tmp[:, 2:3], -0.5, 1.5, ALU.mult, ALU.add), n + 8)
                link(nc.vector.tensor_tensor(out(0), tmp[:, 1:2], tmp[:, 2:3], ALU.mult), n + 9)
                last = nc.vector.scalar_tensor_tensor(out(1), mv[:, 0:1], -1.0, out(0), ALU.mult, ALU.mult)
                if done is not None:
                    last.then_inc(done, 1)

            def out1(i):
                return co[:, i:i + 1]

            def stat1(b, c):
                last = nc.vector.bn_stats(st1[:, c, :], img[b][:, 4 * c:4 * c + 4, :].rearrange("p a w -> p (a w)"))
                if c == CH - 1:
                    last.then_inc(taken, 1)

            def add(n, b, c):
                dve.wait_ge(conv, OPEN + n * CH + c + 1)
                rows = img[b][:, 4 * c:4 * c + 4, :].rearrange("p a w -> p (a w)")
                nc.vector.tensor_tensor(rows, psC[:, c % 2, :], rows, ALU.add).then_inc(added, 1)
                dve.wait_ge(added, n * CH + c + 1 + CREDIT)
                last = nc.vector.bn_stats(st2[:, c, :], rows)
                if c == CH - 1:
                    last.then_inc(taken, 1)

            def second(n, v):
                base = stat_ap
                coefs(st2, v, lambda i: view(base, n * 2 + i, [[1, 1]]), None)

            def body(n, b, v, prep=True):
                if prep:
                    dve.wait_ge(img_in[1 - b], 32 * ((n + 1) // 2) + 32)
                for c in range(CH // 2):
                    add(n, b, c)
                    if prep:
                        stat1(1 - b, 2 * c)
                        stat1(1 - b, 2 * c + 1)
                if prep:
                    dve.wait_ge(nlo, OPEN + n * 4 + 4)
                    coefs(st1, v, out1, coef)
                for c in range(CH // 2, CH):
                    add(n, b, c)
                second(n, v + 1 if prep else v)

            stat_ap = a["norm2"][:]
            nc.vector.sem_inc(added, CREDIT)
            dve.wait_ge(img_in[0], 32)
            for c in range(CH):
                stat1(0, c)
            coefs(st1, 1, out1, coef)
            for j in pairs(dve, N):
                body(2 * j, 0, j * 4 + 2)
                body(2 * j + 1, 1, j * 4 + 4)
            body(N - 2, 0, 2 * N - 2)
            body(N - 1, 1, 2 * N, prep=False)

        @block.tensor
        def _(pe):
            pe.sem_inc(conv, OPEN)
            def group_sum(v):
                pe.wait_ge(mom, v)
                nc.tensor.matmul(psG[:], a["gmask"][:], mv[:], start=True, stop=True).then_inc(gsum, 1)

            def chunks(n, b, c0, c1):
                with pe.Fori(c0 // 2, c1 // 2) as h:
                    for p in range(2):
                        c = h * 2 + p
                        pe.wait_ge(nlo, OPEN + n * 4 + 4)
                        pe.wait_ge(added, n * CH + c - 2 + CREDIT + 1)
                        t = 0
                        for si in range(3):
                            for kw in range(4):
                                for wi, di in SPLITS:
                                    last = nc.tensor.matmul(
                                        psC[:, p, :], a["Wc"][:, wi, si * 4 + kw, :],
                                        view(xn[b][:], di * (RP + 2) * FR_W + (c * 4 + si) * FR_W + kw, [[FR_W, 4], [1, HW]]),
                                        start=(t == 0), stop=(t == 35))
                                    t += 1
                        last.then_inc(conv, 1)

            def body(n, b, v, prep=True):
                chunks(n, b, 0, CH // 2)
                if prep:
                    group_sum(v)
                chunks(n, b, CH // 2, CH)
                group_sum(v + 1 if prep else v)

            group_sum(1)
            for j in pairs(pe, N):
                body(2 * j, 0, j * 4 + 2)
                body(2 * j + 1, 1, j * 4 + 4)
            body(N - 2, 0, 2 * N - 2)
            body(N - 1, 1, 2 * N, prep=False)


def stage2(nc, a, N):
    ctx = ExitStack()
    with ctx:
        def sb(name, shape, dt=F32):
            return ctx.enter_context(nc.sbuf_tensor(name, shape, dt))

        def sem(name):
            return ctx.enter_context(nc.semaphore(name))

        def ps(name, shape):
            return ctx.enter_context(nc.psum_tensor(name, shape, F32))

        xin = sb("xin", [P, 16 * HW])
        eo = sb("eo", [P, 2, 8, 4, 16])
        xn = sb("xn2", [P, 2, 32, 2, 128], F16)
        ux = [sb(f"ux{b}", [P, 2, 2, 512], F16) for b in range(2)]
        f32 = sb("f32", [P, 2, 512])
        fx = [sb(f"fx{b}", [P, 2, 2, 512], F16) for b in range(2)]
        y = sb("y", [P, 16, 2, HALF], F16)
        ct = [sb(f"ct{b}", [P, 2, Y1W], F16) for b in range(2)]
        sh = sb("sh", [P, 2, Y1W], F16)
        cw = [sb(f"cw{b}", [P, 2, 2, 4, 128], F16) for b in range(2)]
        g = sb("g", [P, GN_])
        gp = sb("gp", [P, GW])
        gs = sb("gs", [P, 2, 2, GW], F16)
        gt = [[sb(f"gt{u}{k}", [P, 2, 32 * TP], F16) for k in range(KC)] for u in range(2)]
        yt = [[sb(f"yt{u}{k}", [P, 2, HALF], F16) for k in range(KC)] for u in range(2)]
        res = sb("res", [P, 16, HW])
        co = sb("co2", [P, 2])
        bank = ps("bank", [P, 6, 512])
        pd = ps("pd", [P, 2, 512])

        zpad = sem("pads_zeroed")
        x_in = sem("x_in")
        co_set = sem("norm2_fetched")
        n32 = sem("normed2_f32")
        fold = sem("even_odd_done")
        nhi = sem("normed2_hi")
        nlo = sem("normed2_lo")
        expand = sem("expand_done")
        uhi = sem("expand_hi")
        ulo = sem("expand_lo")
        fwd = sem("forward_done")
        fm = sem("filtered")
        fhi = sem("filtered_hi")
        flo = sem("filtered_lo")
        inv = sem("inverse_done")
        yhi = sem("y_hi")
        ylo = sem("y_lo")
        y_out = sem("y_stored")
        c_in = [sem("tiles_in0"), sem("tiles_in1")]
        sh_in = sem("shifted_in")
        cwr = sem("bands_built")
        c3 = sem("dw3_done")
        c5 = sem("dw5_done")
        x1 = sem("x1_summed")
        gl = sem("gelu_done")
        gate = [sem("gate3_done"), sem("gate5_done")]
        ghi = [sem("gate3_hi"), sem("gate5_hi")]
        glo = [sem("gate3_lo"), sem("gate5_lo")]
        g_out = sem("gates_stored")
        d_in = [[sem(f"operands_in{u}{k}") for k in range(KC)] for u in range(2)]
        d_used = [[sem(f"operands_used{u}{k}") for k in range(KC)] for u in range(2)]
        added = sem("projection_added")
        r_in = sem("residual_in")
        r_out = sem("residual_out")
        IM = C * HW * HW

        block = ctx.enter_context(nc.Block())

        def image_rows(ap, n, h, row, rows, step):
            return dram(ap, n * IM + (64 * h + row) * HW, [[HW * HW, C], [step * HW, rows], [1, HW]])

        def held(eng):
            eng.wait_ge(zpad, 3)

        def folded(part, q, s):
            return [view(xn[:], part * 8192 + (q * 8 + 4 * s) * 256 + e * 128, [[16, 8], [256, 4], [1, 16]]) for e in range(2)]

        def slots(eng, run):
            run(0, 0, 0)
            run(1, 0, 1)
            with eng.Fori(1, SLOTS // 2) as j:
                run(2 * j, j, 0)
                run(2 * j + 1, j, 1)
            run(SLOTS, SLOTS // 2, 0)
            run(SLOTS + 1, SLOTS // 2, 1)

        def live(s):
            if not isinstance(s, int):
                return True, True, True
            return s < SLOTS, 1 <= s <= SLOTS, s >= 2

        def schedule(eng, norm, filt, depth, proj):
            def image(n, first, last):
                filt(n, 1)
                depth(n, 0, None if first else n - 1, None)
                filt(n, 2)
                depth(n, 1, None, None if last else n + 1)
                if not last:
                    filt(n + 1, 0)
                depth(n, 2, None, None)

            with eng.Fori(0, 4) as q:
                norm(0, q)
            filt(0, 0)
            image(0, True, False)
            if N > 2:
                with eng.Fori(1, N - 1) as n:
                    image(n, False, False)
            image(N - 1, False, True)
            with eng.Fori(0, 4) as j:
                for p in range(2):
                    proj(N - 1, j, p)

        @block.sync
        def _(sp):
            sp.sem_inc(y_out, OPEN)
            sp.sem_inc(g_out, OPEN)
            sp.wait_ge(zpad, 3)

            def norm(n, q):
                sp.wait_ge(fold, n * 8 + q * 2 + OPEN)
                for h in range(2):
                    sp.dma_start(view(xin[:], 0, [[HW, 16], [1, HW]], C, C * h),
                                 image_rows(a["xs"], n, h, 16 * q, 16, 1)).then_inc(x_in, 16)

            def filt(n, k):
                m = n * KC + k
                sp.wait_ge(ylo, OPEN + m * 2 * SLOTS + 2 * SLOTS)
                for h in range(2):
                    sp.dma_start(dram(a["Y1"], (n % 2) * Y1N + k * C * 32 * Y1W + 1 + (16 * h + 1) * TP,
                                      [[32 * Y1W, C], [Y1W, 32], [1, HALF]]),
                                 view(y[:], 0, [[HALF, 32], [1, HALF]], C, C * h)).then_inc(y_out, 16)

            def tiles(n, k, gi, p):
                sp.wait_ge(c5, (n * KC + k) * 8 + gi - 1 + CREDIT)
                sp.dma_start(ct[p][:], dram(a["Y1"], (n % 2) * Y1N + (k * 8 + gi) * P * 2 * Y1W,
                                            [[2 * Y1W, 16], [32 * Y1W, 8], [1, 2 * Y1W]])).then_inc(c_in[p], 16)

            def shifted(n, k, gi, p, use):
                sp.wait_ge(x1, (n * KC + k) * 8 + gi + OPEN)
                sp.wait_ge(c_in[p], use * 16)
                for cl in range(4):
                    start = TP + 1 - TP * (cl // 2) - cl % 2
                    sp.dma_start(view(sh[:], 0, [[1, Y1W + GN_]], 32, 32 * cl),
                                 view(ct[p][:], start, [[1, Y1W + GN_]], 32, 32 * cl)).then_inc(sh_in, 16)

            def gates_out(n, k, gi):
                for t in range(2):
                    sp.wait_ge(glo[t], OPEN + (n * KC + k) * 8 + gi + 1)
                    sp.dma_start(dram(a["Gd"], (n % 2) * GDN + (k * P + t * C + gi * 8) * 32 * GW,
                                      [[2 * GW, 16], [32 * GW, 8], [1, 2 * GW]]),
                                 view(gs[:], t * 2 * GW, [[1, 2 * GW]])).then_inc(g_out, 16)

            def proj(n, j, p):
                ih, il = j // 2, j % 2
                for u in range(2):
                    ij = ih * 8 + p * 4 + il * 2 + u
                    for k in range(KC):
                        sp.wait_ge(d_used[u][k], n * 8 + j * 2 + p + OPEN)
                        sp.dma_start(gt[u][k][:], dram(a["Gd"], (n % 2) * GDN + k * P * 32 * GW + ij * 2 * GW + ih * TP + p,
                                                       [[32 * GW, P], [GW, 2], [1, 32 * TP]])).then_inc(d_in[u][k], 16)
                        for h in range(2):
                            sp.dma_start(view(yt[u][k][:], 0, [[HALF, 2], [1, HALF]], C, C * h),
                                         dram(a["Y1"], (n % 2) * Y1N + k * C * 32 * Y1W + ij * 2 * Y1W + 1 + (16 * h + 1) * TP,
                                              [[32 * Y1W, C], [Y1W, 2], [1, HALF]])).then_inc(d_in[u][k], 16)

            def depth(n, k, pn, nn):
                m = n * KC + k
                with sp.Fori(0, 3) as j:
                    for p in range(2):
                        gi = 2 * j + p
                        if pn is not None and p == 0:
                            sp.wait_ge(g_out, OPEN + 32 * NG * n)
                        shifted(n, k, gi + 1, 1 - p, m * 4 + j + 1 + p)
                        if pn is not None:
                            proj(pn, j, p)
                        if nn is not None and p == 0:
                            norm(nn, j)
                        tiles(n, k, gi + 2, p)
                        gates_out(n, k, gi)
                shifted(n, k, 7, 1, m * 4 + 4)
                if pn is not None:
                    proj(pn, 3, 0)
                if nn is not None:
                    norm(nn, 3)
                gates_out(n, k, 6)
                if pn is not None:
                    proj(pn, 3, 1)
                gates_out(n, k, 7)

            def ahead(n, k):
                sp.wait_ge(y_out, OPEN + (n * KC + k) * 32 + 32)
                tiles(n, k, 0, 0)
                tiles(n, k, 1, 1)
                shifted(n, k, 0, 0, (n * KC + k) * 4 + 1)

            def filt_ahead(n, k):
                if not (isinstance(n, int) and n == 0 and k == 0):
                    ahead(*((n, k - 1) if k else (n - 1, KC - 1)))
                filt(n, k)

            def last_depth(n, k, pn, nn):
                if isinstance(n, int) and n == N - 1 and k == KC - 1:
                    ahead(n, k)
                depth(n, k, pn, nn)

            def last_proj(n, j, p):
                sp.wait_ge(g_out, OPEN + 32 * NG * N)
                proj(n, j, p)

            schedule(sp, norm, filt_ahead, last_depth, last_proj)
            sp.wait_ge(r_out, OPEN + 32 * 4 * N)

        @block.gpsimd
        def _(pool):
            nc.gpsimd.memset(y[:], 0.0).then_inc(zpad, 1)
            nc.gpsimd.memset(gs[:], 0.0).then_inc(zpad, 1)
            nc.gpsimd.memset(gp[:], 0.0).then_inc(zpad, 1)
            pool.sem_inc(x1, OPEN)
            pool.sem_inc(glo[0], OPEN)
            pool.sem_inc(glo[1], OPEN)
            pool.sem_inc(flo, OPEN)
            pool.sem_inc(nlo, OPEN)

            def norm(n, q):
                for s in range(2):
                    pool.wait_ge(nhi, n * 8 + q * 2 + s + 1)
                    for e, (dst, hi) in enumerate(zip(folded(1, q, s), folded(0, q, s))):
                        last = nc.gpsimd.tensor_tensor(dst, eo[:, e], hi, ALU.subtract)
                    last.then_inc(nlo, 1)

            def filt(n, k):
                m = n * KC + k
                with pool.Fori(0, SLOTS // 2) as j:
                    for p in range(2):
                        pool.wait_ge(fhi, m * SLOTS + j * 2 + p + 1)
                        nc.gpsimd.tensor_tensor(fx[p][:, 1], f32[:], fx[p][:, 0], ALU.subtract).then_inc(flo, 1)

            def depth(n, k, pn, nn):
                m = n * KC + k
                with pool.Fori(0, 4) as j:
                    for p in range(2):
                        G = m * 8 + j * 2 + p
                        pool.wait_ge(sh_in, G * 64 + 64)
                        pool.wait_ge(gate[1], OPEN + G)
                        nc.gpsimd.tensor_tensor(g[:], sh[:, 0, 0:GN_], sh[:, 1, 0:GN_], ALU.add).then_inc(x1, 1)
                        for t in range(2):
                            pool.wait_ge(ghi[t], G + 1)
                            nc.gpsimd.tensor_tensor(gs[:, t, 1], gp[:], gs[:, t, 0], ALU.subtract).then_inc(glo[t], 1)
                        if nn is not None and p == 0:
                            norm(nn, j)

            schedule(pool, norm, filt, depth, lambda n, j, p: None)

        @block.scalar
        def _(act):
            act.sem_inc(r_out, OPEN)
            act.wait_ge(zpad, 3)

            def norm(n, q):
                nc.scalar.activation(co[:], view(a["norm2"][:], n * 2, [[1, 2]]), ACT.Copy).then_inc(co_set, 1)
                act.wait_ge(co_set, n * 4 + q + 1)
                act.wait_ge(x_in, (n * 4 + q) * 32 + 32)
                nc.scalar.activation(xin[:], xin[:], ACT.Identity, bias=co[:, 1:2], scale=co[:, 0:1]).then_inc(n32, 1)
                for s in range(2):
                    act.wait_ge(fold, n * 8 + q * 2 + s + 1 + OPEN)
                    held(act)
                    for e, dst in enumerate(folded(0, q, s)):
                        last = nc.scalar.activation(dst, eo[:, e], ACT.Copy)
                    last.then_inc(nhi, 1)

            def filt(n, k):
                m = n * KC + k
                act.wait_ge(y_out, OPEN + m * 32)

                def run(s, j, q):
                    ex, fo, iv = live(s)
                    if ex:
                        act.wait_ge(expand, m * SLOTS + s + 1)
                        act.wait_ge(fwd, m * SLOTS + s - 1 + CREDIT)
                        nc.scalar.activation(ux[q][:, 0], bank[:, 0:2, :], ACT.Copy).then_inc(uhi, 1)
                    if fo:
                        act.wait_ge(fm, OPEN + m * SLOTS + s)
                        act.wait_ge(inv, m * SLOTS + s - 2 + CREDIT)
                        nc.scalar.activation(fx[1 - q][:, 0], f32[:], ACT.Copy).then_inc(fhi, 1)
                    if iv:
                        act.wait_ge(inv, m * SLOTS + s - 1 + CREDIT)
                        held(act)
                        for pw in range(2):
                            nc.scalar.activation(
                                view(y[:], (j - 1) * 4 * TP + q * 16 + pw * 8, [[2 * HALF, 16], [TP, 4], [1, 8]]),
                                bank[:, 4 + pw, :].rearrange("p (x a b) -> p x a b", x=16, a=4),
                                ACT.Copy).then_inc(yhi, 1)

                slots(act, run)

            def proj(n, j, p):
                if p == 0:
                    act.wait_ge(r_out, OPEN + (n * 4 + j) * 32)
                    for h in range(2):
                        act.dma_start(view(res[:], 0, [[HW, 16], [1, HW]], C, C * h),
                                      image_rows(a["xs"], n, h, j, 16, 4)).then_inc(r_in, 16)
                else:
                    act.wait_ge(added, n * 16 + j * 4 + 4 + CREDIT)
                    for h in range(2):
                        act.dma_start(image_rows(a["out"], n, h, j, 16, 4),
                                      view(res[:], 0, [[HW, 16], [1, HW]], C, C * h)).then_inc(r_out, 16)

            def depth(n, k, pn, nn):
                m = n * KC + k
                with act.Fori(0, 4) as j:
                    for p in range(2):
                        G = m * 8 + j * 2 + p
                        if pn is not None and p == 0:
                            proj(pn, j, 0)
                        act.wait_ge(x1, G + 1 + OPEN)
                        held(act)
                        nc.scalar.activation(g[:], g[:], ACT.Gelu, scale=view(a["w1g"][:], k * 8 + j * 2 + p, [[1, 1]])).then_inc(gl, 1)
                        act.wait_ge(g_out, OPEN + G * 32)
                        for t in range(2):
                            act.wait_ge(gate[t], OPEN + G + 1)
                            nc.scalar.activation(gs[:, t, 0], gp[:], ACT.Copy).then_inc(ghi[t], 1)
                        if nn is not None and p == 0:
                            norm(nn, j)
                    if pn is not None:
                        proj(pn, j, 1)

            schedule(act, norm, filt, depth, proj)

        @block.vector
        def _(dve):
            dve.sem_inc(added, CREDIT)
            for s in (fold, gate[0], gate[1], ulo, fm, ylo):
                dve.sem_inc(s, OPEN)
            dve.wait_ge(zpad, 3)

            def bands(k, gi, p):
                nc.vector.tensor_tensor(view(cw[p][:], 0, [[128, 16], [8, 16], [1, 8]]),
                                        view(a["tabs"][:], (k * 8 + gi) * 256, [[16, 16], [1, 16], [0, 8]]),
                                        view(a["cmask"][:], 0, [[0, 16], [0, 16], [1, 8]]), ALU.mult).then_inc(cwr, 1)

            def norm(n, q):
                dve.wait_ge(n32, n * 4 + q + 1)
                for s in range(2):
                    dve.wait_ge(nlo, n * 8 + q * 2 + s + OPEN)
                    x = view(xin[:], 4 * s * 16, [[HW, 8], [16, 4], [1, 16]])
                    mirror = view(xin[:], 15 * HW + 4 * s * 16 + 15, [[-HW, 8], [16, 4], [-1, 16]])
                    nc.vector.tensor_tensor(eo[:, 0], x, mirror, ALU.add)
                    nc.vector.tensor_tensor(eo[:, 1], x, mirror, ALU.subtract).then_inc(fold, 1)

            def filt(n, k):
                m = n * KC + k

                def run(s, j, q):
                    ex, fo, iv = live(s)
                    if ex:
                        dve.wait_ge(uhi, m * SLOTS + s + 1)
                        nc.vector.tensor_tensor(ux[q][:, 1], bank[:, 0:2, :], ux[q][:, 0], ALU.subtract).then_inc(ulo, 1)
                    if fo:
                        dve.wait_ge(fwd, m * SLOTS + s + CREDIT)
                        dve.wait_ge(flo, OPEN + m * SLOTS + s - 1)
                        for mh in range(2):
                            last = nc.vector.tensor_tensor(
                                f32[:, mh, :].rearrange("p (a c) -> p a c", c=C),
                                bank[:, 2 + mh, :].rearrange("p (a c) -> p a c", c=C),
                                view(a["wf"][:], mh * HID + k * C, [[0, 8], [1, C]]), ALU.mult)
                        last.then_inc(fm, 1)
                    if iv:
                        for pw in range(2):
                            dve.wait_ge(yhi, (m * SLOTS + s - 2) * 2 + pw + 1)
                            at = (j - 1) * 4 * TP + q * 16 + pw * 8
                            hi, lo = (view(y[:], part * HALF + at, [[2 * HALF, 16], [TP, 4], [1, 8]]) for part in range(2))
                            nc.vector.tensor_tensor(lo, bank[:, 4 + pw, :].rearrange("p (x a b) -> p x a b", x=16, a=4), hi,
                                                    ALU.subtract).then_inc(ylo, 1)

                slots(dve, run)

            def proj(n, j, p):
                if p == 0:
                    dve.wait_ge(r_in, (n * 4 + j) * 32 + 32)
                for u in range(2):
                    dve.wait_ge(d_used[u][KC - 1], OPEN + n * 8 + j * 2 + p + 1)
                    rows = view(res[:], 2 * p + u, [[HW, 16], [4, 32]])
                    nc.vector.tensor_tensor(rows, pd[:, u, :].rearrange("p (a b) -> p a b", b=32), rows,
                                            ALU.add).then_inc(added, 1)

            def depth(n, k, pn, nn):
                m = n * KC + k
                with dve.Fori(0, 4) as j:
                    for p in range(2):
                        G = m * 8 + j * 2 + p
                        dve.wait_ge(c5, G + CREDIT)
                        bands(k, j * 2 + p + 1, 1 - p)
                        dve.wait_ge(gl, G + 1)
                        for t, done in ((0, c3), (1, c5)):
                            dve.wait_ge(done, G + 1 + (CREDIT if t else 0))
                            dve.wait_ge(glo[1 - t], OPEN + G + t)
                            nc.vector.tensor_tensor(gp[:, 0:GN_].rearrange("p (b n) -> p b n", b=3),
                                                    bank[:, 3 * t:3 * t + 3, 0:NB],
                                                    g[:].rearrange("p (b n) -> p b n", b=3), ALU.mult).then_inc(gate[t], 1)
                        if pn is not None:
                            proj(pn, j, p)
                        if nn is not None and p == 0:
                            norm(nn, j)

            bands(0, 0, 0)
            schedule(dve, norm, filt, depth, proj)

        @block.tensor
        def _(pe):
            for s in (fwd, inv, c5):
                pe.sem_inc(s, CREDIT)
            for u in range(2):
                for k in range(KC):
                    pe.sem_inc(d_used[u][k], OPEN)

            def filt(n, k):
                m = n * KC + k
                before = m - 1
                pe.wait_ge(nlo, n * 8 + 8 + OPEN)
                pe.wait_ge(gate[1], (before * 8 if not isinstance(before, int) or before > 0 else 0) + OPEN)

                def run(s, j, q):
                    ex, fo, iv = live(s)
                    if ex:
                        pe.wait_ge(ulo, OPEN + m * SLOTS + s)
                        for r in range(2):
                            for pw in range(4):
                                for t, (wi, di) in enumerate(SPLITS):
                                    last = nc.tensor.matmul(
                                        bank[:, r, pw * 128:(pw + 1) * 128],
                                        view(xn[:], di * 8192 + ((j * 8 + q * 4 + pw) * 2 + r) * 128, [[1, 128]]),
                                        a["Win"][:, wi, k, :], start=(t == 0), stop=(t == 2))
                        last.then_inc(expand, 1)
                    if fo:
                        pe.wait_ge(ulo, OPEN + m * SLOTS + s)
                        pe.wait_ge(fm, OPEN + m * SLOTS + s - 1)
                        for mh in range(2):
                            for t, (wi, di) in enumerate(SPLITS):
                                last = nc.tensor.matmul(bank[:, 2 + mh, :], a["Bf"][:, wi, mh, :],
                                                        ux[1 - q][:, di, mh, :], start=(t == 0), stop=(t == 2))
                        last.then_inc(fwd, 1)
                    if iv:
                        pe.wait_ge(flo, OPEN + m * SLOTS + s - 1)
                        pe.wait_ge(ylo, OPEN + (m * SLOTS + s - 2) * 2)
                        for pw in range(4):
                            t = 0
                            for mh in range(2):
                                for wi, di in SPLITS:
                                    last = nc.tensor.matmul(
                                        view(bank[:], (4 + pw // 2) * 512 + (pw % 2) * 4, [[8, 64], [1, 4]]),
                                        fx[q][:, di, mh, pw * 128:(pw + 1) * 128], a["Bi"][:, wi, mh, :],
                                        start=(t == 0 and pw % 2 == 0), stop=(t == 5), skip_group_check=True)
                                    t += 1
                        last.then_inc(inv, 1)

                slots(pe, run)

            def proj(n, j, p):
                for u in range(2):
                    it = n * 16 + j * 4 + p * 2 + u
                    pe.wait_ge(added, it - 1 + CREDIT)
                    for k in range(KC):
                        pe.wait_ge(d_in[u][k], (n * 8 + j * 2 + p) * 48 + 48)
                        for wi, di in SPLITS:
                            nc.tensor.matmul(pd[:, u, :], a["W3"][:, wi, k, :], view(yt[u][k][:], di * HALF, [[TP, 16], [1, 32]]),
                                             start=(k == 0 and wi + di == 0), stop=False, skip_group_check=True)
                        for wi, di in SPLITS:
                            for h in range(2):
                                last = nc.tensor.matmul(
                                    pd[C * h:C * h + C, u, :], a["Wg"][:, wi, k, :],
                                    view(gt[u][k][:], (di * 32 + 16 * h) * TP, [[TP, 16], [1, 32]]),
                                    start=False, stop=(k == KC - 1 and wi == 1), skip_group_check=True)
                        last.then_inc(d_used[u][k], 1)

            def depth(n, k, pn, nn):
                m = n * KC + k
                filtered = m + 1 if not (isinstance(n, int) and n == N - 1 and k == KC - 1) else m
                with pe.Fori(0, 4) as j:
                    for p in range(2):
                        G = m * 8 + j * 2 + p
                        if p == 0:
                            pe.wait_ge(ylo, OPEN + (filtered + 1) * SLOTS * 2)
                        pe.wait_ge(c_in[p], (m * 4 + j) * 16 + 16)
                        pe.wait_ge(cwr, G + 1)
                        for x, done in ((0, c3), (1, c5)):
                            pe.wait_ge(gate[x], OPEN + G)
                            t = 0
                            for q in range(4):
                                for wi, di in SPLITS:
                                    for b in range(3):
                                        last = nc.tensor.matmul(
                                            bank[:, 3 * x + b, 0:NB], cw[p][:, wi, x, q, :],
                                            view(ct[p][:], di * Y1W + b * NB + (q // 2) * TP + q % 2, [[1, NB]]),
                                            start=(t == 0), stop=(t == 11))
                                    t += 1
                            last.then_inc(done, 1)
                        if pn is not None:
                            proj(pn, j, p)

            schedule(pe, lambda n, q: None, filt, depth, proj)


def program(nc, a, N):
    ctx = ExitStack()
    with ctx:
        for name, shape, dt in (
            ("Win", [P, 2, KC, 128], F16),
            ("W3", [P, 2, KC, 128], F16),
            ("Wg", [P, 2, KC, 64], F16),
            ("Bf", [P, 2, 2, 128], F16),
            ("Bi", [P, 2, 2, 256], F16),
            ("wf", [P, 2, HID], F32),
            ("w1g", [P, NG], F32),
            ("tabs", [P, NG + 1, 2, 128], F16),
            ("cmask", [P, 8], F16),
            ("norm2", [P, N, 2], F32),
        ):
            a[name] = ctx.enter_context(nc.sbuf_tensor("c_" + name, shape, dt))
        a["ws"] = nc.dram_tensor("ws", (65536,), F32, kind="Internal").ap()
        a["xs"] = nc.dram_tensor("xs", (N * C * HW * HW,), F32, kind="Internal").ap()
        a["Y1"] = nc.dram_tensor("Y1", (2 * Y1N,), F16, kind="Internal").ap()
        a["Gd"] = nc.dram_tensor("Gd", (2 * GDN,), F16, kind="Internal").ap()
        with ExitStack() as early:
            for name, shape, dt in (
                ("Wc", [P, 2, 12, 128], F16),
                ("ident", [P, 128], F32),
                ("gmask", [P, 128], F32),
            ):
                a[name] = early.enter_context(nc.sbuf_tensor("c_" + name, shape, dt))
            stage0(nc, a)
            stage1(nc, a, N)
        stage2(nc, a, N)



def _tile_order():
    return [(2 * ih + il, 2 * jh + jl) for ih in range(2) for jh in range(2) for il in range(2) for jl in range(2)]


def _basis():
    r, w = np.meshgrid(np.arange(16) + 0.5, np.arange(16) + 0.5, indexing="ij")
    even, odd = [], []
    for ky in range(9):
        for kx in range(16):
            if ky in (0, 8) and kx > 8:
                continue
            arg = 2 * np.pi * (kx * r + ky * w) / 16
            other = (16 - kx) % 16 if ky in (0, 8) else kx
            for fs, f in ((even, np.cos(arg)), (odd, np.sin(arg))):
                norm = np.sqrt((f * f).sum())
                if norm > 1e-6:
                    fs.append((f / norm * 4, kx * 9 + ky, other * 9 + ky))
    phi, pos, neg = zip(*(even + odd))
    return np.array(phi), np.array(pos), np.array(neg)


def _split(v):
    hi = v.astype(np.float16)
    return np.stack([hi, (v - hi.astype(np.float64)).astype(np.float16)])


def _layouts(x, L0_conv_gates, L1_conv_w_in, L1_conv_fft_w, L1_conv_w1, L1_conv_w3, L1_conv_w5, L1_conv_w_out):
    N = x.shape[0]
    perm = np.arange(C).reshape(2, 2, 16).transpose(1, 0, 2).reshape(-1)
    d = {}
    d["x"] = np.ascontiguousarray(x[:, perm]).reshape(-1)
    gates = np.asarray(L0_conv_gates).reshape(3, 15, 4, 4)
    row = np.arange(256).reshape(2, P)
    pair = np.stack([(row >> s) & 3 for s in (6, 4, 2, 0)])
    gi = np.arange(4)[:, None, None]
    d["ge"] = np.stack([gates[:, gi + 4 * op, pair] for op in range(2)], 1).transpose(4, 0, 1, 3, 2, 5)
    p = np.arange(P)
    mid = np.stack([(p >> s) & 3 for s in (5, 3, 1)])
    g3 = np.arange(3)[:, None]
    d["go"] = np.concatenate([gates[:, 8 + g3, mid], gates[:, 12 + g3, mid]], 1).transpose(2, 0, 1, 3)
    cross = gates[:, 11].reshape(3, 2, 2, 2, 2)[:, p & 1]
    d["gx"] = cross.transpose(1, 0, 2, 4, 3)
    d["i2"] = (p[:, None] & 1 == np.arange(2)).astype(np.float32)
    d["d_ident"] = np.eye(P, dtype=np.float32)
    grp = (p % C) // 2
    d["d_gmask"] = (grp[:, None] == grp[None]).astype(np.float32) / 4
    d["d_cmask"] = (p[:, None] % 8 == np.arange(8)).astype(np.float16)
    order = _tile_order()
    oi = np.array([o[0] for o in order])
    oj = np.array([o[1] for o in order])
    q = np.arange(4)
    dh = 4 * (q // 2)[None, :, None] + oi[:, None, None] - ((oi + 2) % 4)[None, None, :]
    dw = 4 * (q % 2)[None, :, None] + oj[:, None, None] - ((oj + 2) % 4)[None, None, :]
    def taps(w, size, shift):
        w = np.pad(np.asarray(w).reshape(HID, size, size), ((0, 0), (4, 4), (4, 4)))
        return w[:, dh - shift + 4, dw - shift + 4]
    tab = np.stack([taps(L1_conv_w3, 3, 1), taps(L1_conv_w5, 5, 0)], 2)
    d["tab"] = tab.reshape(NG, 8, 16, 128).transpose(2, 1, 0, 3).reshape(P, NG, 128)
    w1 = np.asarray(L1_conv_w1).reshape(HID)
    d["w1c"] = w1.reshape(KC, C)[:, p % C].T
    d["d_w1g"] = w1.reshape(NG, 8)[:, p % 8].T
    d["win"] = np.asarray(L1_conv_w_in).reshape(HID, C)[:, perm].T.reshape(-1)
    d["wout"] = np.asarray(L1_conv_w_out).reshape(C, 3 * HID)[perm].T.reshape(-1)
    phi, pos, neg = _basis()
    fw = np.asarray(L1_conv_fft_w).reshape(HID, 144)
    d["fw"] = np.stack([fw[:, pos], fw[:, neg]]).reshape(2, HID, 2, P).transpose(3, 2, 0, 1)
    d["d_Bf"] = _split(phi.reshape(2, P, 256)[:, :, :P].transpose(2, 0, 1)).transpose(1, 0, 2, 3)
    tiles = phi.reshape(256, 4, 4, 4, 4)[:, :, oi, :, :]
    tiles = tiles[:, :, np.arange(16), :, oj]
    d["d_Bi"] = _split(tiles.transpose(1, 0, 2, 3).reshape(2, P, 256).transpose(1, 0, 2)).transpose(1, 0, 2, 3)
    return {k: np.ascontiguousarray(v) for k, v in d.items()}, perm, N


def kernel(x, L0_conv_gates, L1_conv_w_in, L1_conv_fft_w, L1_conv_w1, L1_conv_w3, L1_conv_w5, L1_conv_w_out):
    import concourse.bacc as bacc
    from concourse.bass_utils import run_bass_kernel_spmd

    arrays, perm, N = _layouts(x, L0_conv_gates, L1_conv_w_in, L1_conv_fft_w, L1_conv_w1, L1_conv_w3, L1_conv_w5, L1_conv_w_out)
    nc = bacc.Bacc("TRN2", target_bir_lowering=False, num_devices=1)
    a = {k: nc.dram_tensor("in_" + k, v.shape, mybir.dt.from_np(v.dtype), kind="ExternalInput").ap() for k, v in arrays.items()}
    a["out"] = nc.dram_tensor("out_dram", (N * C * HW * HW,), F32, kind="ExternalOutput").ap()
    program(nc, a, N)
    r = run_bass_kernel_spmd(nc, [{"in_" + k: v for k, v in arrays.items()}], core_ids=[0])
    out = r.results[0]["out_dram"].reshape(N, C, HW, HW)
    return out[:, np.argsort(perm)]
```

```python
from contextlib import ExitStack

import concourse.bass as bass
import numpy as np
from concourse import mybir

F32 = mybir.dt.float32
F16 = mybir.dt.float16
ALU = mybir.AluOpType
ACT = mybir.ActivationFunctionType

P = 128
C = 64
HW = 128
RP = HW // 2
HID = 192
KC = HID // C
EPS = 1e-5
FR_W = 132
XS_W = 130
CH = 16
TP = 33
HALF = 16 * TP
Y1W = 1124
GN_ = 33 * TP
GW = 1090
NB = GN_ // 3
NG = HID // 8
SLOTS = 8
OPEN = 1
LEAD = 3
CREDIT = 2
Y1N = HID * 32 * Y1W
GDN = KC * P * 32 * GW
SPLITS = ((0, 0), (0, 1), (1, 0))


def view(ap, off, dims, parts=None, p0=0):
    step = ap.ap[0][0]
    n = ap.ap[0][1] if parts is None else parts
    return bass.AP(tensor=ap.tensor, offset=ap.offset + p0 * step + off, ap=[[step, n]] + [list(d) for d in dims])


def dram(ap, off, dims):
    return bass.AP(tensor=ap.tensor, offset=ap.offset + off, ap=[list(d) for d in dims])


def pairs(eng, N):
    if N > 2:
        with eng.Fori(0, N // 2 - 1) as j:
            yield j


def stage0(nc, a):
    ctx = ExitStack()
    with ctx:
        def sb(name, shape, dt=F32):
            return ctx.enter_context(nc.sbuf_tensor(name, shape, dt))

        def sem(name):
            return ctx.enter_context(nc.semaphore(name))

        ge = sb("ge", [P, 3, 2, 2, 4, 4])
        go = sb("go", [P, 3, 6, 4])
        gx = sb("gx", [P, 3, 4, 2])
        i2 = sb("i2", [P, 2])
        K = sb("K", [P, 2, 2, 256])
        R = sb("R", [P, 4, 128])
        Cm = sb("Cm", [P, 128])
        o16 = sb("o16", [P, 2, 16])
        o64 = sb("o64", [P, 2, 64])
        S = sb("S", [P, 2, 256])
        T = sb("T", [P, 2, 256])
        Wo = sb("Wo", [C, 1024])
        Wt = sb("Wt", [C, 12, 2, 2, 2, 2, 16])
        tab = sb("tab", [P, NG, 128])
        zero = sb("zero", [P, 96 * 36], F16)
        win32 = sb("win32", [P, KC, 128])
        wout32 = sb("wout32", [P, KC, 128])
        wg32 = sb("wg32", [P, KC, 64])
        w1c = sb("w1c", [P, KC])
        fw = sb("fw", [P, 2, 2, HID])
        psT = ctx.enter_context(nc.psum_tensor("psT", [P, 2, 256], F32))
        psS = ctx.enter_context(nc.psum_tensor("psS", [P, 2, 256], F32))
        psW = ctx.enter_context(nc.psum_tensor("psW", [P, 12, 128], F32))

        gates_in = sem("gates_in")
        consts_in = sem("consts_in")
        blocks_in = sem("blocks_in")
        zeroed = sem("zeroed")
        step = sem("dve_step")
        mats = sem("mats_built")
        pe_step = sem("pe_step")
        ev = sem("state_evacuated")
        s_out = sem("state_stored")
        s_in = sem("weight_loaded")
        wt_done = sem("taps_laid_out")
        wtr = sem("taps_transposed")
        whi = sem("conv_weight_hi")
        zst = sem("frames_zeroed")
        cst = sem("const_hi")
        n_gates, n_consts, n_blocks = 4, 12, 8

        block = ctx.enter_context(nc.Block())

        @block.sync
        def _(sp):
            sp.dma_start(ge[:], a["ge"]).then_inc(gates_in, 16)
            sp.dma_start(go[:], a["go"]).then_inc(gates_in, 16)
            sp.dma_start(gx[:], a["gx"]).then_inc(gates_in, 16)
            sp.dma_start(i2[:], a["i2"]).then_inc(gates_in, 16)
            sp.dma_start(a["ident"][:], a["d_ident"]).then_inc(consts_in, 16)
            sp.dma_start(a["gmask"][:], a["d_gmask"]).then_inc(consts_in, 16)
            sp.dma_start(tab[:], a["tab"]).then_inc(consts_in, 16)
            sp.dma_start(a["cmask"][:], a["d_cmask"]).then_inc(consts_in, 16)
            sp.dma_start(a["id16"][:], a["d_id16"]).then_inc(consts_in, 16)
            sp.dma_start(a["Bf"][:], a["d_Bf"]).then_inc(consts_in, 16)
            sp.dma_start(a["Bi"][:], a["d_Bi"]).then_inc(consts_in, 16)
            sp.dma_start(fw[:], a["fw"]).then_inc(consts_in, 16)
            sp.dma_start(a["w1g"][:], a["d_w1g"]).then_inc(consts_in, 16)
            sp.dma_start(w1c[:], a["w1c"]).then_inc(consts_in, 16)
            for t in range(2):
                sp.dma_start(view(wg32[:], 0, [[64, KC], [1, 64]], C, C * t),
                             dram(a["wout"], t * HID * C, [[C, C], [C * C, KC], [1, C]])).then_inc(consts_in, 16)
            sp.wait_ge(zeroed, 2)
            for h in range(2):
                for k in range(KC):
                    sp.dma_start(view(win32[:], k * 128 + C * h, [[1, C]], C, C * h),
                                 dram(a["win"], k * C, [[HID, C], [1, C]])).then_inc(blocks_in, 16)
                sp.dma_start(view(wout32[:], C * h, [[128, KC], [1, 64]], C, C * h),
                             dram(a["wout"], 2 * HID * C, [[C, C], [C * C, KC], [1, C]])).then_inc(blocks_in, 16)
            sp.wait_ge(zeroed, 3)
            rows = HID * 32 // 64
            for par in range(2):
                for off in (0, Y1W - 34):
                    sp.dma_start(dram(a["Y1"], par * Y1N + off, [[Y1W * rows, 64], [Y1W, rows], [1, 34]]),
                                 view(zero[:], 0, [[34, rows], [1, 34]], 64)).then_inc(zst, 16)
            sp.wait_ge(ev, 13)
            sp.dma_start(dram(a["ws"], 0, [[256, P], [P * 256, 2], [1, 256]]), S[:]).then_inc(s_out, 16)
            sp.wait_ge(s_out, 16)
            for u in range(2):
                for t in range(2):
                    sp.dma_start(view(Wo[:], 0, [[1, 1024]], 16, 32 * u + 16 * t),
                                 dram(a["ws"], (32 * t + 16 * u) * 1024, [[1024, 16], [1, 1024]])).then_inc(s_in, 16)
            sp.wait_ge(zst, 64)

        @block.gpsimd
        def _(pool):
            nc.gpsimd.memset(win32[:], 0.0).then_inc(zeroed, 1)
            nc.gpsimd.memset(wout32[:], 0.0).then_inc(zeroed, 1)
            nc.gpsimd.memset(zero[:], 0.0).then_inc(zeroed, 1)

        @block.vector
        def _(dve):
            n = [0]

            def link(ins):
                n[0] += 1
                ins.then_inc(step, 1)
                dve.wait_ge(step, n[0])

            def outer(out, off, x, xoff, y, yoff, nx, ny, outs=None):
                so, sx, sy, b = outs or (0, 0, 0, 1)
                return nc.vector.tensor_tensor(view(out[:], off, [[so, b], [ny, nx], [1, ny]]),
                                               view(x[:], xoff, [[sx, b], [1, nx], [0, ny]]),
                                               view(y[:], yoff, [[sy, b], [0, nx], [1, ny]]), ALU.mult)

            link(nc.vector.memset(S[:], 0.0))
            nc.vector.memset(S[0:1, 0, 0:1], 1.0).then_inc(ev, 1)
            link(nc.vector.memset(Wt[:], 0.0))
            dve.wait_ge(gates_in, 16 * n_gates)
            for r in range(3):
                if r:
                    dve.wait_ge(pe_step, 4 * r)
                for op in range(2):
                    g0 = (r * 2 + op) * 32
                    link(outer(o16, 0, ge, g0, ge, g0 + 4, 4, 4, (16, 16, 16, 2)))
                    link(outer(o64, 0, o16, 0, ge, g0 + 8, 16, 4, (64, 16, 16, 2)))
                    outer(K, op * 512, o64, 0, ge, g0 + 12, 64, 4, (256, 64, 16, 2)).then_inc(mats, 1)
                    dve.wait_ge(mats, 4 * r + op + 1)
                g0 = r * 24
                link(outer(o16, 0, go, g0, go, g0 + 4, 4, 4))
                link(outer(o64, 0, o16, 0, go, g0 + 8, 16, 4))
                outer(R, 0, o64, 0, gx, r * 8, 64, 2, (128, 0, 2, 4)).then_inc(mats, 1)
                dve.wait_ge(mats, 4 * r + 3)
                link(outer(o16, 0, go, g0 + 12, go, g0 + 16, 4, 4))
                link(outer(o64, 0, o16, 0, go, g0 + 20, 16, 4))
                outer(Cm, 0, o64, 0, i2, 0, 64, 2).then_inc(mats, 1)
                for q, (dst, src) in enumerate(((T, psT), (S, psS), (T, psT), (S, psS))):
                    dve.wait_ge(pe_step, 4 * r + q + 1)
                    if q == 3 and r < 2:
                        nc.vector.tensor_scalar(dst[:], src[:], 0.0, None, ALU.max).then_inc(ev, 1)
                    else:
                        nc.vector.tensor_copy(dst[:], src[:]).then_inc(ev, 1)
            dve.wait_ge(consts_in, 16 * n_consts)
            dve.wait_ge(blocks_in, 16 * n_blocks)
            link(nc.vector.tensor_tensor(fw[:, :, 0, :], fw[:, :, 0, :], fw[:, :, 1, :], ALU.add))
            nc.vector.tensor_scalar(a["wf"][:], fw[:, :, 0, :], 0.5 / 16, None, ALU.mult).then_inc(cst, 1)
            for k in range(KC):
                link(nc.vector.tensor_scalar(wout32[:, k, :], wout32[:, k, :], w1c[:, k:k + 1], None, ALU.mult))
            for t32, hl in ((win32, a["Win"]), (wout32, a["W3"]), (wg32, a["Wg"])):
                link(nc.vector.tensor_copy(hl[:, 0], t32[:]))
                nc.vector.tensor_tensor(hl[:, 1], t32[:], hl[:, 0], ALU.subtract).then_inc(cst, 1)
            for part in range(2):
                for at, g0, g1 in ((0, 0, NG), (NG, 0, 1)):
                    dst = view(a["tabs"][:], at * 256 + part * 128, [[256, g1 - g0], [1, 128]])
                    if part == 0:
                        link(nc.vector.tensor_copy(dst, tab[:, g0:g1, :]))
                    else:
                        nc.vector.tensor_tensor(dst, tab[:, g0:g1, :], view(a["tabs"][:], at * 256, [[256, g1 - g0], [1, 128]]),
                                                ALU.subtract).then_inc(cst, 1)
            dve.wait_ge(s_in, 64)
            for si in range(3):
                for po in range(2):
                    for pi in range(2):
                        for t in range(2):
                            kh = 2 * (si - 1) + pi - po + 2 - t
                            if 0 <= kh < 4:
                                last = nc.vector.tensor_copy(
                                    view(Wt[:], si * 1024 + po * 128 + pi * 64 + t * 16, [[256, 4], [32, 2], [1, 16]]),
                                    view(Wo[:], t * 32 * 16 + kh * 4, [[1, 4], [256, 2], [16, 16]]))
            last.then_inc(wt_done, 1)
            dve.wait_ge(whi, 1)
            nc.vector.tensor_tensor(a["Wc"][:, 1], psW[:], a["Wc"][:, 0], ALU.subtract).then_inc(cst, 1)

        @block.scalar
        def _(act):
            act.wait_ge(wtr, 1)
            nc.scalar.activation(a["Wc"][:, 0], psW[:], ACT.Copy).then_inc(whi, 1)

        @block.tensor
        def _(pe):
            for r in range(3):
                for q in range(4):
                    pe.wait_ge(ev, 4 * r + q + 1)
                    pe.wait_ge(mats, 4 * r + q + 1)
                    if q < 2:
                        src, dst = (S, psT) if q == 0 else (T, psS)
                        for m in range(2):
                            for kb in range(2):
                                last = nc.tensor.matmul(dst[:, m, :], src[:, kb, m * 128:(m + 1) * 128], K[:, q, kb, :],
                                                        start=(kb == 0), stop=(kb == 1))
                    elif q == 2:
                        for bo in range(2):
                            for kb in range(2):
                                for b in range(2):
                                    last = nc.tensor.matmul(psT[:, bo, kb * 128:(kb + 1) * 128],
                                                            S[:, kb, b * 128:(b + 1) * 128], R[:, 2 * b + bo, :],
                                                            start=(b == 0), stop=(b == 1))
                    else:
                        for m in range(2):
                            for cb in range(2):
                                last = nc.tensor.matmul(psS[:, m, cb * 128:(cb + 1) * 128],
                                                        T[:, cb, m * 128:(m + 1) * 128], Cm[:], start=True, stop=True)
                    last.then_inc(pe_step, 1)
            pe.wait_ge(wt_done, 1)
            pe.wait_ge(consts_in, 16 * n_consts)
            for tk in range(12):
                for po in range(2):
                    last = nc.tensor.matmul(psW[:, tk, po * C:(po + 1) * C],
                                            view(Wt[:], tk * 256 + po * 128, [[1, 128]]),
                                            a["ident"][0:C, 0:C], start=True, stop=True, is_transpose=True)
            last.then_inc(wtr, 1)


def stage1(nc, a, N):
    ctx = ExitStack()
    with ctx:
        def sb(name, shape, dt=F32):
            return ctx.enter_context(nc.sbuf_tensor(name, shape, dt))

        def sem(name):
            return ctx.enter_context(nc.semaphore(name))

        raw = sb("raw", [P, RP, XS_W])
        img = [sb(f"img{b}", [P, RP, HW]) for b in range(2)]
        xn = [sb(f"xn{b}", [P, 2, RP + 2, FR_W], F16) for b in range(2)]
        st1 = sb("st1", [P, CH, 6])
        st2 = sb("st2", [P, CH, 6])
        mv = sb("mv", [P, 2])
        tmp = sb("tmp", [P, 4])
        sd = sb("sd", [P, 1])
        co = sb("co", [P, 2])
        zcol = sb("zcol", [P, 16, 1])
        psC = ctx.enter_context(nc.psum_tensor("psC", [P, 2, 512], F32))
        psG = ctx.enter_context(nc.psum_tensor("psG", [P, 2], F32))

        img_in = [sem("img_in0"), sem("img_in1")]
        raw_in = sem("raw_in")
        img_out = [sem("img_out0"), sem("img_out1")]
        pads = sem("frames_cleared")
        step = sem("dve_step1")
        mom = sem("moments_ready")
        gsum = sem("group_sums")
        vready = sem("variance_ready")
        root = sem("root_ready")
        coef = sem("norm_coef")
        n32 = sem("normed_f32")
        nhi = sem("normed_hi")
        lows = sem("low_halves")
        nlo = sem("normed_lo")
        taken = sem("stats_taken")
        conv = sem("conv_done")
        added = sem("residual_added")

        block = ctx.enter_context(nc.Block())
        xi, xs = a["x"], a["xs"]
        IM = C * HW * HW

        def load_img(eng, n, b):
            for par in range(2):
                eng.dma_start(view(img[b][:], 0, [[HW, RP], [1, HW]], C, C * par),
                              dram(xi, n * IM + par * HW, [[HW * HW, C], [2 * HW, RP], [1, HW]])).then_inc(img_in[b], 16)

        def load_raw(eng, n):
            for par in range(2):
                for u in range(2):
                    eng.dma_start(view(raw[:], 1 - u, [[XS_W, RP], [1, HW]], 32, C * par + 32 * u),
                                  dram(xi, n * IM + u * 32 * HW * HW + par * HW,
                                       [[HW * HW, 32], [2 * HW, RP], [1, HW]])).then_inc(raw_in, 16)

        @block.sync
        def _(sp):
            sp.sem_inc(img_out[0], OPEN)
            sp.sem_inc(img_out[1], OPEN)
            def prep(n, b, m):
                sp.wait_ge(img_out[b], OPEN + m * 32)
                if not isinstance(n, int) or n:
                    sp.wait_ge(mom, 2 * n - 1)
                load_img(sp, n, b)
                sp.wait_ge(nlo, OPEN + n * 4)
                load_raw(sp, n)

            def post(n, b):
                sp.wait_ge(added, n * CH + CH + CREDIT)
                for par in range(2):
                    sp.dma_start(dram(xs, n * IM + par * HW, [[HW * HW, C], [2 * HW, RP], [1, HW]]),
                                 view(img[b][:], 0, [[HW, RP], [1, HW]], C, C * par)).then_inc(img_out[b], 16)

            sp.wait_ge(pads, 4)
            prep(0, 0, 0)
            for j in pairs(sp, N):
                prep(2 * j + 1, 1, j)
                post(2 * j, 0)
                prep(2 * j + 2, 0, j + 1)
                post(2 * j + 1, 1)
            prep(N - 1, 1, N // 2 - 1)
            post(N - 2, 0)
            post(N - 1, 1)
            sp.wait_ge(img_out[0], OPEN + 32 * (N // 2))
            sp.wait_ge(img_out[1], OPEN + 32 * (N // 2))

        @block.gpsimd
        def _(pool):
            pool.sem_inc(nlo, OPEN)
            nc.gpsimd.memset(raw[:], 0.0).then_inc(pads, 1)
            nc.gpsimd.memset(xn[0][:], 0.0).then_inc(pads, 1)
            nc.gpsimd.memset(xn[1][:], 0.0).then_inc(pads, 1)
            nc.gpsimd.memset(zcol[:], 0.0).then_inc(pads, 1)
            pool.wait_ge(pads, 4)

            def prep(n, b):
                for q in range(4):
                    pool.wait_ge(nlo, OPEN + n * 4 + q)
                    pool.wait_ge(nhi, n * 4 + q + 1)
                    rows = slice(16 * q, 16 * q + 16)
                    frame = slice(16 * q + 1, 16 * q + 17)
                    nc.gpsimd.tensor_tensor(xn[b][:, 1, frame, 1:130], raw[:, rows, 0:129], xn[b][:, 0, frame, 1:130],
                                            ALU.subtract).then_inc(lows, 1)
                    pool.wait_ge(lows, n * 4 + q + 1)
                    for part in range(4):
                        col = 1 if part % 2 == 0 else 129
                        edge = slice(32 * part, 32 * part + 32)
                        for border in (raw[edge, rows, col - 1:col], xn[b][edge, 0, frame, col:col + 1], xn[b][edge, 1, frame, col:col + 1]):
                            last = nc.gpsimd.tensor_tensor(border, zcol[edge], zcol[edge], ALU.add)
                    last.then_inc(nlo, 1)

            prep(0, 0)
            for j in pairs(pool, N):
                prep(2 * j + 1, 1)
                prep(2 * j + 2, 0)
            prep(N - 1, 1)

        @block.scalar
        def _(act):
            def sqrt_step(v):
                act.wait_ge(vready, v)
                nc.scalar.activation(sd[:], tmp[:, 0:1], ACT.Sqrt).then_inc(root, 1)

            def prep(n, b, v):
                sqrt_step(v)
                act.wait_ge(coef, n + 1)
                act.wait_ge(raw_in, n * 64 + 64)
                if not isinstance(n, int) or n:
                    act.wait_ge(conv, OPEN + (n - 1) * CH)
                for q in range(4):
                    rows = slice(16 * q, 16 * q + 16)
                    nc.scalar.activation(raw[:, rows, 0:129], raw[:, rows, 0:129], ACT.Identity,
                                         bias=co[:, 1:2], scale=co[:, 0:1]).then_inc(n32, 1)
                    act.wait_ge(n32, n * 4 + q + 1)
                    nc.scalar.activation(xn[b][:, 0, 16 * q + 1:16 * q + 17, 1:130], raw[:, rows, 0:129],
                                         ACT.Copy).then_inc(nhi, 1)

            prep(0, 0, 1)
            for j in pairs(act, N):
                prep(2 * j + 1, 1, j * 4 + 2)
                sqrt_step(j * 4 + 3)
                prep(2 * j + 2, 0, j * 4 + 4)
                sqrt_step(j * 4 + 5)
            prep(N - 1, 1, 2 * N - 2)
            sqrt_step(2 * N - 1)
            sqrt_step(2 * N)

        @block.vector
        def _(dve):
            def link(ins, n):
                ins.then_inc(step, 1)
                dve.wait_ge(step, n)

            LINKS = 9

            def moments(stats, v):
                n = (v - 1) * LINKS
                dve.wait_ge(taken, v)
                nc.vector.memset(tmp[:, 3:4], 0.0)
                link(nc.vector.bn_aggr(mv[:], stats[:]), n + 1)
                link(nc.vector.tensor_tensor(tmp[:, 1:2], mv[:, 0:1], mv[:, 0:1], ALU.mult), n + 2)
                nc.vector.tensor_tensor(mv[:, 1:2], mv[:, 1:2], tmp[:, 1:2], ALU.add).then_inc(mom, 1)

            def coefs(v, out, done):
                n = (v - 1) * LINKS
                dve.wait_ge(gsum, v)
                link(nc.vector.tensor_copy(mv[:], psG[:]), n + 3)
                link(nc.vector.tensor_tensor(tmp[:, 1:2], mv[:, 0:1], mv[:, 0:1], ALU.mult), n + 4)
                link(nc.vector.tensor_tensor(tmp[:, 0:1], mv[:, 1:2], tmp[:, 1:2], ALU.subtract), n + 5)
                nc.vector.tensor_scalar(tmp[:, 0:1], tmp[:, 0:1], EPS, None, ALU.add).then_inc(vready, 1)
                dve.wait_ge(root, v)
                link(nc.vector.reciprocal(tmp[:, 1:2], sd[:]), n + 6)
                link(nc.vector.scalar_tensor_tensor(tmp[:, 2:3], tmp[:, 1:2], tmp[:, 1:2], tmp[:, 0:1], ALU.mult, ALU.mult), n + 7)
                link(nc.vector.tensor_scalar(tmp[:, 2:3], tmp[:, 2:3], -0.5, 1.5, ALU.mult, ALU.add), n + 8)
                link(nc.vector.tensor_tensor(out(0), tmp[:, 1:2], tmp[:, 2:3], ALU.mult), n + 9)
                last = nc.vector.scalar_tensor_tensor(out(1), mv[:, 0:1], -1.0, out(0), ALU.mult, ALU.mult)
                if done is not None:
                    last.then_inc(done, 1)

            def out1(i):
                return co[:, i:i + 1]

            def stat1(b, c):
                last = nc.vector.bn_stats(st1[:, c, :], img[b][:, 4 * c:4 * c + 4, :].rearrange("p a w -> p (a w)"))
                if c == CH - 1:
                    last.then_inc(taken, 1)

            def add(n, b, c):
                dve.wait_ge(conv, OPEN + n * CH + c + 1)
                rows = img[b][:, 4 * c:4 * c + 4, :].rearrange("p a w -> p (a w)")
                nc.vector.tensor_tensor(rows, psC[:, c % 2, :], rows, ALU.add).then_inc(added, 1)
                dve.wait_ge(added, n * CH + c + 1 + CREDIT)
                last = nc.vector.bn_stats(st2[:, c, :], rows)
                if c == CH - 1:
                    last.then_inc(taken, 1)

            def second(n, v):
                coefs(v, lambda i: view(stat_ap, n * 2 + i, [[1, 1]]), None)

            def body(n, b, v, before=None, prep=True):
                for c in range(CH):
                    if c == 2 and before is not None:
                        second(n - 1, before)
                    if c == CH // 4 and prep:
                        dve.wait_ge(img_in[1 - b], 32 * ((n + 1) // 2) + 32)
                    if c == CH // 2 + 2 and prep:
                        dve.wait_ge(nlo, OPEN + n * 4 + 4)
                        coefs(v, out1, coef)
                    add(n, b, c)
                    if prep and CH // 4 <= c < CH // 2:
                        for i in range(4):
                            stat1(1 - b, 4 * (c - CH // 4) + i)
                    if c == CH // 2 - 1 and prep:
                        moments(st1, v)
                moments(st2, v + 1 if prep else v)

            stat_ap = a["norm2"][:]
            nc.vector.sem_inc(added, CREDIT)
            dve.wait_ge(img_in[0], 32)
            for c in range(CH):
                stat1(0, c)
            moments(st1, 1)
            coefs(1, out1, coef)
            body(0, 0, 2)
            if N > 2:
                with dve.Fori(0, N // 2 - 1) as j:
                    body(2 * j + 1, 1, j * 4 + 4, j * 4 + 3)
                    body(2 * j + 2, 0, j * 4 + 6, j * 4 + 5)
            body(N - 1, 1, 2 * N, 2 * N - 1, prep=False)
            second(N - 1, 2 * N)

        @block.tensor
        def _(pe):
            pe.sem_inc(conv, OPEN)
            def group_sum(v):
                pe.wait_ge(mom, v)
                nc.tensor.matmul(psG[:], a["gmask"][:], mv[:], start=True, stop=True).then_inc(gsum, 1)

            def chunks(n, b, c0, c1):
                with pe.Fori(c0 // 2, c1 // 2) as h:
                    for p in range(2):
                        c = h * 2 + p
                        pe.wait_ge(nlo, OPEN + n * 4 + 4)
                        pe.wait_ge(added, n * CH + c - 2 + CREDIT + 1)
                        t = 0
                        for si in range(3):
                            for kw in range(4):
                                for wi, di in SPLITS:
                                    last = nc.tensor.matmul(
                                        psC[:, p, :], a["Wc"][:, wi, si * 4 + kw, :],
                                        view(xn[b][:], di * (RP + 2) * FR_W + (c * 4 + si) * FR_W + kw, [[FR_W, 4], [1, HW]]),
                                        start=(t == 0), stop=(t == 35))
                                    t += 1
                        last.then_inc(conv, 1)

            def body(n, b, v, before=None, prep=True):
                chunks(n, b, 0, 2)
                if before is not None:
                    group_sum(before)
                chunks(n, b, 2, CH // 2 + 2)
                if prep:
                    group_sum(v)
                chunks(n, b, CH // 2 + 2, CH)

            group_sum(1)
            body(0, 0, 2)
            if N > 2:
                with pe.Fori(0, N // 2 - 1) as j:
                    body(2 * j + 1, 1, j * 4 + 4, j * 4 + 3)
                    body(2 * j + 2, 0, j * 4 + 6, j * 4 + 5)
            body(N - 1, 1, 2 * N, 2 * N - 1, prep=False)
            group_sum(2 * N)


def stage2(nc, a, N):
    ctx = ExitStack()
    with ctx:
        def sb(name, shape, dt=F32):
            return ctx.enter_context(nc.sbuf_tensor(name, shape, dt))

        def sem(name):
            return ctx.enter_context(nc.semaphore(name))

        def ps(name, shape):
            return ctx.enter_context(nc.psum_tensor(name, shape, F32))

        xin = sb("xin", [P, 16 * HW])
        eo = sb("eo", [P, 2, 8, 4, 16])
        xn = sb("xn2", [P, 2, 32, 2, 128], F16)
        even = sb("even", [P, 512])
        fx = [sb(f"fx{b}", [P, 2, 2, 512], F16) for b in range(2)]
        y = sb("y", [P, 16, 2, HALF], F16)
        ct = [sb(f"ct{b}", [P, 2, Y1W], F16) for b in range(2)]
        sh = sb("sh", [P, 2, Y1W], F16)
        cw = [sb(f"cw{b}", [P, 2, 2, 4, 128], F16) for b in range(2)]
        g = [sb(f"g{b}", [P, GW]) for b in range(2)]
        gp = [sb(f"gp{t}", [P, GW]) for t in range(2)]
        f32 = [view(x[:], 0, [[512, 2], [1, 512]]) for x in g]
        tmp = [view(x[:], 0, [[512, 2], [1, 512]]) for x in gp]
        gs = sb("gs", [P, 2, 2, GW], F16)
        gt = [[sb(f"gt{u}{k}", [P, 2, 32 * TP], F16) for k in range(KC)] for u in range(2)]
        yt = [[sb(f"yt{u}{k}", [P, 2, HALF], F16) for k in range(KC)] for u in range(2)]
        res = sb("res", [P, 16, HW])
        co = sb("co2", [P, 2])
        bank = ps("bank", [P, 6, 512])
        pd = ps("pd", [P, 2, 512])

        zpad = sem("pads_zeroed")
        x_in = sem("x_in")
        co_set = sem("norm2_fetched")
        n32 = sem("normed2_f32")
        fold = sem("even_odd_done")
        nhi = sem("normed2_hi")
        nlo = sem("normed2_lo")
        turned = sem("pixels_on_partitions")
        uhi = sem("pixels_hi")
        ulo = sem("pixels_lo")
        fwd = sem("forward_done")
        xhi = sem("spectra_hi")
        xlo = sem("spectra_lo")
        expand = sem("expand_done")
        fm = sem("filtered")
        fhi = sem("filtered_hi")
        flo = sem("filtered_lo")
        inv = sem("inverse_done")
        yev = sem("y_even_copied")
        ysum = sem("y_unfolded")
        yhi = sem("y_hi")
        ylo = [sem("y_lo_0"), sem("y_lo_1")]
        y_out = sem("y_stored")
        c_in = [sem("tiles_in0"), sem("tiles_in1")]
        sh_in = sem("shifted_in")
        cwr = sem("bands_built")
        c3 = sem("dw3_done")
        c5 = sem("dw5_done")
        x1 = sem("x1_summed")
        gl = sem("gelu_done")
        gate = [sem("gate3_done"), sem("gate5_done")]
        ghi = [sem("gate3_hi"), sem("gate5_hi")]
        glo = [sem("gate3_lo"), sem("gate5_lo")]
        g_out = sem("gates_stored")
        d_in = [[sem(f"operands_in{u}{k}") for k in range(KC)] for u in range(2)]
        d_used = [[sem(f"operands_used{u}{k}") for k in range(KC)] for u in range(2)]
        added = sem("projection_added")
        r_in = sem("residual_in")
        r_out = sem("residual_out")
        IM = C * HW * HW

        block = ctx.enter_context(nc.Block())

        def image_rows(ap, n, h, row, rows, step):
            return dram(ap, n * IM + (64 * h + row) * HW, [[HW * HW, C], [step * HW, rows], [1, HW]])

        def held(eng):
            eng.wait_ge(zpad, 3)

        def folded(part, q, s):
            return [view(xn[:], part * 8192 + (q * 8 + 4 * s) * 256 + e * 128, [[16, 8], [256, 4], [1, 16]]) for e in range(2)]

        def slots(eng, run, drain=None):
            for s in range(4):
                run(s, s // 2, s % 2)
            with eng.Fori(2, SLOTS // 2) as j:
                run(2 * j, j, 0)
                run(2 * j + 1, j, 1)
            if drain:
                drain()
            for s in range(SLOTS, SLOTS + 4):
                run(s, s // 2, s % 2)

        def live(s, lag):
            return not isinstance(s, int) or 0 <= s - lag < SLOTS

        def turned_bank(q):
            return bank[:, 4 * q:4 * q + 2, :]

        def fwd_bank(q):
            return pd[:] if q else bank[:, 2:4, :]

        def patches(part, j, q):
            return view(xn[:], part * 8192 + (j * 8 + q * 4 - 4) * 256, [[128, 2], [256, 4], [1, 128]])

        def inv_bank(q, e):
            return pd[:, e, :] if q else bank[:, 4 + e, :]

        def placed(j, q, part, mirror):
            at = (j - 2) * 4 * TP + q * 16 + part * HALF + mirror * 2 * TP
            return view(y[:], at, [[2 * HALF, 16], [TP, 2], [1, 16]])

        def filtered(n, k):
            return n * KC + k + (0 if isinstance(n, int) and n == N - 1 and k == KC - 1 else 1)

        def mirrored(ap):
            return view(ap, 31 * 16 + 3, [[-16, 32], [4, 4], [-1, 4]])

        def unfolded(q, e):
            return tmp[q][:, e, :].rearrange("p (x a b) -> p x a b", x=16, a=2)

        def proj_part(eng, proj, n, k, steps):
            with eng.Fori(0, steps) as j:
                for u in range(2):
                    proj(n, k, j, u)

        def schedule(eng, norm, spec, filt, depth, proj, fetch=None, steps=4):
            def image(n, first, last):
                filt(n, 1)
                depth(n, 0, None if first else n - 1, None)
                if fetch and not last:
                    fetch(n + 1)
                filt(n, 2)
                depth(n, 1, None if first else n - 1, None if last else n + 1)
                if not last:
                    spec(n + 1)
                    filt(n + 1, 0)
                depth(n, 2, None, None)

            with eng.Fori(0, 4) as q:
                for s in range(2):
                    norm(0, q, s)
            spec(0)
            filt(0, 0)
            image(0, True, False)
            if N > 2:
                with eng.Fori(1, N - 1) as n:
                    image(n, False, False)
            image(N - 1, False, True)
            for k in range(2):
                proj_part(eng, proj, N - 1, k, steps)

        @block.sync
        def _(sp):
            sp.sem_inc(y_out, OPEN)
            sp.sem_inc(g_out, OPEN)
            sp.wait_ge(zpad, 3)

            def norm(n, q, s):
                if s:
                    return
                sp.wait_ge(fold, n * 8 + q * 2 + OPEN)
                for h in range(2):
                    sp.dma_start(view(xin[:], 0, [[HW, 16], [1, HW]], C, C * h),
                                 image_rows(a["xs"], n, h, 16 * q, 16, 1)).then_inc(x_in, 16)

            def filt(n, k):
                m = n * KC + k
                for e in range(2):
                    sp.wait_ge(ylo[e], LEAD + m * SLOTS + SLOTS)
                store(n, k, 0)
                if isinstance(n, int) and n == 0 and k == 0:
                    store(n, k, 1)

            def store(n, k, h):
                sp.dma_start(dram(a["Y1"], (n % 2) * Y1N + k * C * 32 * Y1W + 1 + (16 * h + 1) * TP,
                                  [[32 * Y1W, C], [Y1W, 32], [1, HALF]]),
                             view(y[:], 0, [[HALF, 32], [1, HALF]], C, C * h)).then_inc(y_out, 16)

            def tiles(n, k, gi, p, stored=True):
                sp.wait_ge(c5, (n * KC + k) * 8 + gi - 1 + CREDIT)
                if not stored:
                    sp.wait_ge(y_out, OPEN + (n * KC + k) * 32 + 32)
                sp.dma_start(ct[p][:], dram(a["Y1"], (n % 2) * Y1N + (k * 8 + gi) * P * 2 * Y1W,
                                            [[2 * Y1W, 16], [32 * Y1W, 8], [1, 2 * Y1W]])).then_inc(c_in[p], 16)

            def shifted(n, k, gi, p, use):
                sp.wait_ge(x1, (n * KC + k) * 8 + gi + OPEN)
                sp.wait_ge(c_in[p], use * 16)
                for cl in range(4):
                    start = TP + 1 - TP * (cl // 2) - cl % 2
                    sp.dma_start(view(sh[:], 0, [[1, Y1W + GN_]], 32, 32 * cl),
                                 view(ct[p][:], start, [[1, Y1W + GN_]], 32, 32 * cl)).then_inc(sh_in, 16)

            def gates_out(n, k, gi):
                for t in range(2):
                    sp.wait_ge(glo[t], OPEN + (n * KC + k) * 8 + gi + 1)
                    sp.dma_start(dram(a["Gd"], (n % 2) * GDN + (k * P + t * C + gi * 8) * 32 * GW,
                                      [[2 * GW, 16], [32 * GW, 8], [1, 2 * GW]]),
                                 view(gs[:], t * 2 * GW, [[1, 2 * GW]])).then_inc(g_out, 16)

            def proj(n, k, j, u):
                ij = k * 8 + (j % 2) * 4 + (j // 2) * 2 + u
                for c in range(KC):
                    sp.wait_ge(d_used[u][c], n * 8 + k * 4 + j + OPEN)
                    sp.dma_start(gt[u][c][:], dram(a["Gd"], (n % 2) * GDN + c * P * 32 * GW + ij * 2 * GW + k * TP + j % 2,
                                                   [[32 * GW, P], [GW, 2], [1, 32 * TP]])).then_inc(d_in[u][c], 16)
                    for h in range(2):
                        sp.dma_start(view(yt[u][c][:], 0, [[HALF, 2], [1, HALF]], C, C * h),
                                     dram(a["Y1"], (n % 2) * Y1N + c * C * 32 * Y1W + ij * 2 * Y1W + 1 + (16 * h + 1) * TP,
                                          [[32 * Y1W, C], [Y1W, 2], [1, HALF]])).then_inc(d_in[u][c], 16)

            def depth(n, k, pn, nn):
                m = n * KC + k
                with sp.Fori(0, 3) as j:
                    for p in range(2):
                        gi = 2 * j + p
                        if pn is not None:
                            proj(pn, k, j + p, 1 - p)
                        shifted(n, k, gi + 1, 1 - p, m * 4 + j + 1 + p)
                        if nn is not None and p == 1:
                            norm(nn, j + 1, 0)
                        tiles(n, k, gi + 2, p)
                        gates_out(n, k, gi)
                if pn is not None:
                    proj(pn, k, 3, 1)
                shifted(n, k, 7, 1, m * 4 + 4)
                if k < KC - 1:
                    store(n, k + 1, 1)
                elif not (isinstance(n, int) and n == N - 1):
                    store(n + 1, 0, 1)
                gates_out(n, k, 6)
                gates_out(n, k, 7)

            def ahead(n, k):
                tiles(n, k, 0, 0, stored=False)
                tiles(n, k, 1, 1)
                shifted(n, k, 0, 0, (n * KC + k) * 4 + 1)

            def filt_ahead(n, k):
                if k and not (isinstance(n, int) and n == 0):
                    if k == 1:
                        sp.wait_ge(g_out, OPEN + 32 * NG * n)
                    proj(n - 1, k - 1, 0, 0)
                if not (isinstance(n, int) and n == 0 and k == 0):
                    ahead(*((n, k - 1) if k else (n - 1, KC - 1)))
                filt(n, k)

            def last_depth(n, k, pn, nn):
                if isinstance(n, int) and n == N - 1 and k == KC - 1:
                    ahead(n, k)
                depth(n, k, pn, nn)

            def last_proj(n, k, j, u):
                sp.wait_ge(g_out, OPEN + 32 * NG * N)
                proj(n, k, j, u)

            schedule(sp, norm, lambda n: None, filt_ahead, last_depth, last_proj, lambda n: norm(n, 0, 0))
            sp.wait_ge(r_out, OPEN + 32 * 4 * N)

        @block.gpsimd
        def _(pool):
            nc.gpsimd.memset(view(y[:], 32, [[HALF, 32], [TP, 16], [1, 1]]), 0.0).then_inc(zpad, 1)
            for t in range(2):
                nc.gpsimd.memset(gp[t][:, GN_:GW], 0.0).then_inc(zpad, 1)
            pool.sem_inc(x1, OPEN)
            pool.sem_inc(glo[0], OPEN)
            pool.sem_inc(glo[1], OPEN)
            pool.sem_inc(flo, CREDIT)
            pool.sem_inc(ylo[0], LEAD)
            pool.sem_inc(nlo, OPEN)

            def norm(n, q, s):
                pool.wait_ge(nhi, n * 8 + q * 2 + s + 1)
                for e, (dst, hi) in enumerate(zip(folded(1, q, s), folded(0, q, s))):
                    last = nc.gpsimd.tensor_tensor(dst, eo[:, e], hi, ALU.subtract)
                last.then_inc(nlo, 1)

            def filt(n, k):
                m = n * KC + k

                def run(s, j, q):
                    if live(s, 0):
                        pool.wait_ge(fhi, m * SLOTS + s + 1)
                        nc.gpsimd.tensor_tensor(fx[q][:, 1], f32[q], fx[q][:, 0], ALU.subtract).then_inc(flo, 1)
                    if live(s, 4):
                        pool.wait_ge(yhi, (m * SLOTS + s - 4) * 2 + 1)
                        nc.gpsimd.tensor_tensor(placed(j, q, 1, 0), unfolded(q, 0), placed(j, q, 0, 0),
                                                ALU.subtract).then_inc(ylo[0], 1)

                slots(pool, run)

            def depth(n, k, pn, nn):
                m = n * KC + k
                with pool.Fori(0, 4) as j:
                    for p in range(2):
                        G = m * 8 + j * 2 + p
                        pool.wait_ge(sh_in, G * 64 + 64)
                        pool.wait_ge(gate[1], CREDIT + G - 1)
                        nc.gpsimd.tensor_tensor(g[p][:, 0:GN_], sh[:, 0, 0:GN_], sh[:, 1, 0:GN_], ALU.add).then_inc(x1, 1)
                        for t in range(2):
                            if nn is not None and p == t == 1:
                                norm(nn, j, 1)
                            pool.wait_ge(ghi[t], G + 1)
                            nc.gpsimd.tensor_tensor(gs[:, t, 1], gp[t][:], gs[:, t, 0], ALU.subtract).then_inc(glo[t], 1)
                        if nn is not None and p == 0:
                            norm(nn, j, 0)

            schedule(pool, norm, lambda n: None, filt, depth, lambda n, k, j, u: None)

        @block.scalar
        def _(act):
            act.sem_inc(r_out, OPEN)
            act.wait_ge(zpad, 3)

            def scale(n, q):
                nc.scalar.activation(co[:], view(a["norm2"][:], n * 2, [[1, 2]]), ACT.Copy).then_inc(co_set, 1)
                act.wait_ge(co_set, n * 4 + q + 1)
                act.wait_ge(x_in, (n * 4 + q) * 32 + 32)
                nc.scalar.activation(xin[:], xin[:], ACT.Identity, bias=co[:, 1:2], scale=co[:, 0:1]).then_inc(n32, 1)

            def norm(n, q, s, scaled=False):
                if s == 0 and not scaled:
                    scale(n, q)
                act.wait_ge(fold, n * 8 + q * 2 + s + 1 + OPEN)
                held(act)
                for e, dst in enumerate(folded(0, q, s)):
                    last = nc.scalar.activation(dst, eo[:, e], ACT.Copy)
                last.then_inc(nhi, 1)

            def spec(n):
                def run(s, j, q):
                    if live(s, 0):
                        act.wait_ge(turned, n * SLOTS + s + 1)
                        act.wait_ge(fwd, n * SLOTS + s - 1 + CREDIT)
                        nc.scalar.activation(fx[q][:, 0], turned_bank(q), ACT.Copy).then_inc(uhi, 1)
                    if live(s, 1):
                        act.wait_ge(fwd, n * SLOTS + s + CREDIT)
                        held(act)
                        nc.scalar.activation(patches(0, j, q), fwd_bank(1 - q).rearrange("p e (x f) -> p e x f", x=4),
                                             ACT.Copy).then_inc(xhi, 1)

                slots(act, run)

            def filt(n, k):
                m = n * KC + k
                act.wait_ge(y_out, OPEN + m * 32)

                def run(s, j, q):
                    if live(s, 4):
                        act.wait_ge(ysum, m * SLOTS + s - 3 + CREDIT)
                        held(act)
                        for e in range(2):
                            nc.scalar.activation(placed(j, q, 0, e), unfolded(q, e), ACT.Copy).then_inc(yhi, 1)
                    if live(s, 3):
                        act.wait_ge(inv, m * SLOTS + s - 2 + CREDIT)
                        act.wait_ge(ysum, m * SLOTS + s - 3 + CREDIT)
                        nc.scalar.activation(even[:], inv_bank(1 - q, 0), ACT.Copy).then_inc(yev, 1)
                    if live(s, 0):
                        act.wait_ge(fm, m * SLOTS + s + 1 + CREDIT)
                        act.wait_ge(inv, m * SLOTS + s - 1 + CREDIT)
                        nc.scalar.activation(fx[q][:, 0], f32[q], ACT.Copy).then_inc(fhi, 1)

                slots(act, run)

            def residual_in(n, i):
                act.wait_ge(r_out, OPEN + (n * 4 + i) * 32)
                for h in range(2):
                    act.dma_start(view(res[:], 0, [[HW, 16], [1, HW]], C, C * h),
                                  image_rows(a["xs"], n, h, i, 16, 4)).then_inc(r_in, 16)

            def residual_out(n, i):
                act.wait_ge(added, n * 16 + i * 4 + 4 + CREDIT)
                for h in range(2):
                    act.dma_start(image_rows(a["out"], n, h, i, 16, 4),
                                  view(res[:], 0, [[HW, 16], [1, HW]], C, C * h)).then_inc(r_out, 16)

            def proj(n, k, j, u):
                if u == 0:
                    residual_in(n, 2 * k + j)
                else:
                    residual_out(n, 2 * k + j)

            def depth(n, k, pn, nn):
                m = n * KC + k

                def group(j, p):
                    G = m * 8 + j * 2 + p
                    act.wait_ge(x1, G + 1 + OPEN)
                    held(act)
                    nc.scalar.activation(g[p][:, 0:GN_], g[p][:, 0:GN_], ACT.Gelu,
                                         scale=view(a["w1g"][:], k * 8 + j * 2 + p, [[1, 1]])).then_inc(gl, 1)
                    if nn is not None and p == 0:
                        scale(nn, j)
                    act.wait_ge(g_out, OPEN + G * 32)
                    for t in range(2):
                        if nn is not None and p == t == 1:
                            norm(nn, j, 1)
                        act.wait_ge(gate[t], CREDIT + G + 1)
                        nc.scalar.activation(gs[:, t, 0], gp[t][:], ACT.Copy).then_inc(ghi[t], 1)
                    if nn is not None and p == 0:
                        norm(nn, j, 0, scaled=True)

                with act.Fori(0, 2) as i:
                    if pn is not None:
                        residual_in(pn, 2 * k + i)
                    for j in range(2):
                        for p in range(2):
                            group(2 * i + j, p)
                    if pn is not None:
                        residual_out(pn, 2 * k + i)

            schedule(act, norm, spec, filt, depth, proj, steps=2)

        @block.vector
        def _(dve):
            for s in (added, ulo, xlo, fm, ysum, gate[0], gate[1]):
                dve.sem_inc(s, CREDIT)
            dve.sem_inc(fold, OPEN)
            dve.sem_inc(ylo[1], LEAD)
            dve.wait_ge(zpad, 3)

            def bands(k, gi, p):
                nc.vector.tensor_tensor(view(cw[p][:], 0, [[128, 16], [8, 16], [1, 8]]),
                                        view(a["tabs"][:], (k * 8 + gi) * 256, [[16, 16], [1, 16], [0, 8]]),
                                        view(a["cmask"][:], 0, [[0, 16], [0, 16], [1, 8]]), ALU.mult).then_inc(cwr, 1)

            def norm(n, q, s):
                dve.wait_ge(n32, n * 4 + q + 1)
                dve.wait_ge(nlo, n * 8 + q * 2 + s + OPEN)
                x = view(xin[:], 4 * s * 16, [[HW, 8], [16, 4], [1, 16]])
                mirror = view(xin[:], 15 * HW + 4 * s * 16 + 15, [[-HW, 8], [16, 4], [-1, 16]])
                nc.vector.tensor_tensor(eo[:, 0], x, mirror, ALU.add)
                nc.vector.tensor_tensor(eo[:, 1], x, mirror, ALU.subtract).then_inc(fold, 1)

            def spec(n):
                def run(s, j, q):
                    if live(s, 0):
                        dve.wait_ge(uhi, n * SLOTS + s + 1)
                        nc.vector.tensor_tensor(fx[q][:, 1], turned_bank(q), fx[q][:, 0], ALU.subtract).then_inc(ulo, 1)
                    if live(s, 1):
                        dve.wait_ge(xhi, n * SLOTS + s)
                        nc.vector.tensor_tensor(patches(1, j, q), fwd_bank(1 - q).rearrange("p e (x f) -> p e x f", x=4),
                                                patches(0, j, q), ALU.subtract).then_inc(xlo, 1)

                slots(dve, run)

            def filt(n, k):
                m = n * KC + k

                def run(s, j, q):
                    if live(s, 0):
                        dve.wait_ge(expand, m * SLOTS + s + 1)
                        dve.wait_ge(flo, m * SLOTS + s - 1 + CREDIT)
                        for mh in range(2):
                            last = nc.vector.tensor_tensor(
                                f32[q][:, mh, :].rearrange("p (a c) -> p a c", c=C),
                                bank[:, 2 * q + mh, :].rearrange("p (a c) -> p a c", c=C),
                                view(a["wf"][:], mh * HID + k * C, [[0, 8], [1, C]]), ALU.mult)
                        last.then_inc(fm, 1)
                    if live(s, 3):
                        dve.wait_ge(yev, m * SLOTS + s - 2)
                        for e in range(2):
                            dve.wait_ge(ylo[e], LEAD + m * SLOTS + s - 4)
                        odd = inv_bank(1 - q, 1)
                        nc.vector.tensor_tensor(tmp[1 - q][:, 0], even[:], odd, ALU.add)
                        nc.vector.tensor_tensor(view(tmp[1 - q], 512, [[16, 32], [4, 4], [1, 4]]),
                                                mirrored(even[:]), mirrored(odd), ALU.subtract).then_inc(ysum, 1)
                    if live(s, 4):
                        dve.wait_ge(yhi, (m * SLOTS + s - 4) * 2 + 2)
                        nc.vector.tensor_tensor(placed(j, q, 1, 1), unfolded(q, 1), placed(j, q, 0, 1),
                                                ALU.subtract).then_inc(ylo[1], 1)

                slots(dve, run)

            def proj(n, k, j, u):
                dve.wait_ge(r_in, (n * 4 + 2 * k + j // 2) * 32 + 32)
                dve.wait_ge(d_used[u][KC - 1], OPEN + n * 8 + k * 4 + j + 1)
                rows = view(res[:], 2 * (j % 2) + u, [[HW, 16], [4, 32]])
                nc.vector.tensor_tensor(rows, pd[:, u, :].rearrange("p (a b) -> p a b", b=32), rows,
                                        ALU.add).then_inc(added, 1)

            def depth(n, k, pn, nn):
                m = n * KC + k
                with dve.Fori(0, 4) as j:
                    for p in range(2):
                        G = m * 8 + j * 2 + p
                        dve.wait_ge(c5, G + CREDIT)
                        bands(k, j * 2 + p + 1, 1 - p)
                        if p == 0:
                            dve.wait_ge(ylo[1], LEAD + (filtered(n, k) + 1) * SLOTS)
                        dve.wait_ge(gl, G + 1)
                        for t, done in ((0, c3), (1, c5)):
                            if nn is not None and p == t == 1:
                                norm(nn, j, 1)
                            dve.wait_ge(done, G + 1 + (CREDIT if t else 0))
                            dve.wait_ge(glo[t], OPEN + G)
                            nc.vector.tensor_tensor(gp[t][:, 0:GN_].rearrange("p (b n) -> p b n", b=3),
                                                    bank[:, 3 * t:3 * t + 3, 0:NB],
                                                    g[p][:, 0:GN_].rearrange("p (b n) -> p b n", b=3), ALU.mult).then_inc(gate[t], 1)
                        if pn is not None:
                            proj(pn, k, j, p)
                        if nn is not None and p == 0:
                            norm(nn, j, 0)

            bands(0, 0, 0)
            schedule(dve, norm, spec, filt, depth, proj)

        @block.tensor
        def _(pe):
            for s in (fwd, inv, c5):
                pe.sem_inc(s, CREDIT)
            for u in range(2):
                for k in range(KC):
                    pe.sem_inc(d_used[u][k], OPEN)

            def spec(n):
                if not isinstance(n, int) or n:
                    pe.wait_ge(gate[1], (n * KC - 1) * 8 + CREDIT)

                def run(s, j, q):
                    if live(s, 0):
                        pe.wait_ge(nlo, n * SLOTS + s + 1 + OPEN)
                        pe.wait_ge(ulo, n * SLOTS + s - 1 + CREDIT)
                        for r in range(2):
                            for pw in range(4):
                                for di in range(2):
                                    last = nc.tensor.matmul(
                                        bank[:, 4 * q + r, pw * 128:(pw + 1) * 128],
                                        view(xn[:], di * 8192 + ((j * 8 + q * 4 + pw) * 2 + r) * 128, [[1, 128]]),
                                        a["id16"][:], start=(di == 0), stop=(di == 1))
                        last.then_inc(turned, 1)
                    if live(s, 1):
                        pe.wait_ge(ulo, n * SLOTS + s + CREDIT)
                        pe.wait_ge(xlo, n * SLOTS + s - 2 + CREDIT)
                        for r in range(2):
                            for pw in range(4):
                                for t, (wi, di) in enumerate(SPLITS):
                                    last = nc.tensor.matmul(fwd_bank(1 - q)[:, r, pw * 128:(pw + 1) * 128],
                                                            fx[1 - q][:, di, r, pw * 128:(pw + 1) * 128],
                                                            a["Bf"][:, wi, r, :], start=(t == 0), stop=(t == 2))
                        last.then_inc(fwd, 1)

                slots(pe, run)

            def filt(n, k):
                m = n * KC + k
                pe.wait_ge(xlo, n * SLOTS + SLOTS + CREDIT)
                if k:
                    pe.wait_ge(gate[1], (m - 1) * 8 + CREDIT)

                def run(s, j, q):
                    if live(s, 0):
                        pe.wait_ge(fm, m * SLOTS + s - 1 + CREDIT)
                        for r in range(2):
                            for pw in range(4):
                                for t, (wi, di) in enumerate(SPLITS):
                                    last = nc.tensor.matmul(
                                        bank[:, 2 * q + r, pw * 128:(pw + 1) * 128],
                                        view(xn[:], di * 8192 + ((j * 8 + q * 4 + pw) * 2 + r) * 128, [[1, 128]]),
                                        a["Win"][:, wi, k, :], start=(t == 0), stop=(t == 2))
                        last.then_inc(expand, 1)
                    if live(s, 2):
                        pe.wait_ge(flo, m * SLOTS + s - 1 + CREDIT)
                        pe.wait_ge(ysum, m * SLOTS + s - 3 + CREDIT)
                        for pw in range(4):
                            for mh in range(2):
                                for t, (wi, di) in enumerate(SPLITS):
                                    last = nc.tensor.matmul(
                                        view(inv_bank(q, mh), pw * 4, [[16, 32], [1, 4]]),
                                        fx[q][:, di, mh, pw * 128:(pw + 1) * 128], a["Bi"][:, wi, mh, :],
                                        start=(t == 0 and pw == 0), stop=(t == 2), skip_group_check=True)
                        last.then_inc(inv, 1)

                def drain():
                    pe.wait_ge(fm, (m + 1) * SLOTS + CREDIT)
                    conv(*((n, k - 1) if k else (n - 1, KC - 1)), 0, 0, 0)

                slots(pe, run, None if isinstance(n, int) and n == 0 and k == 0 else drain)

            def proj(n, k, j, u):
                it = n * 16 + k * 8 + j * 2 + u
                pe.wait_ge(added, it - 1 + CREDIT)
                for c in range(KC):
                    pe.wait_ge(d_in[u][c], (n * 8 + k * 4 + j) * 48 + 48)
                    for wi, di in SPLITS:
                        nc.tensor.matmul(pd[:, u, :], a["W3"][:, wi, c, :], view(yt[u][c][:], di * HALF, [[TP, 16], [1, 32]]),
                                         start=(c == 0 and wi + di == 0), stop=False, skip_group_check=True)
                    for wi, di in SPLITS:
                        for h in range(2):
                            last = nc.tensor.matmul(
                                pd[C * h:C * h + C, u, :], a["Wg"][:, wi, c, :],
                                view(gt[u][c][:], (di * 32 + 16 * h) * TP, [[TP, 16], [1, 32]]),
                                start=False, stop=(c == KC - 1 and wi == 1), skip_group_check=True)
                    last.then_inc(d_used[u][c], 1)

            def conv(n, k, j, p, x):
                G = (n * KC + k) * 8 + j * 2 + p
                if x == 0:
                    pe.wait_ge(c_in[p], ((n * KC + k) * 4 + j) * 16 + 16)
                    pe.wait_ge(cwr, G + 1)
                pe.wait_ge(gate[x], CREDIT + G)
                t = 0
                for q in range(4):
                    for wi, di in SPLITS:
                        for b in range(3):
                            last = nc.tensor.matmul(
                                bank[:, 3 * x + b, 0:NB], cw[p][:, wi, x, q, :],
                                view(ct[p][:], di * Y1W + b * NB + (q // 2) * TP + q % 2, [[1, NB]]),
                                start=(t == 0), stop=(t == 11))
                        t += 1
                last.then_inc(c5 if x else c3, 1)

            def depth(n, k, pn, nn):
                if isinstance(n, int) and n == N - 1 and k == KC - 1:
                    conv(n, k, 0, 0, 0)

                def group(j, p):
                    if p == 0:
                        pe.wait_ge(ysum, CREDIT + (filtered(n, k) + 1) * SLOTS)
                    conv(n, k, j, p, 1)
                    if pn is not None:
                        proj(pn, k, j, p)
                    if not (isinstance(j, int) and j == 3 and p == 1):
                        conv(n, k, j + p, 1 - p, 0)

                with pe.Fori(0, 3) as j:
                    for p in range(2):
                        group(j, p)
                for p in range(2):
                    group(3, p)

            schedule(pe, lambda n, q, s: None, spec, filt, depth, proj)


def program(nc, a, N):
    ctx = ExitStack()
    with ctx:
        for name, shape, dt in (
            ("Win", [P, 2, KC, 128], F16),
            ("W3", [P, 2, KC, 128], F16),
            ("Wg", [P, 2, KC, 64], F16),
            ("id16", [P, 128], F16),
            ("Bf", [P, 2, 2, 128], F16),
            ("Bi", [P, 2, 2, 128], F16),
            ("wf", [P, 2, HID], F32),
            ("w1g", [P, NG], F32),
            ("tabs", [P, NG + 1, 2, 128], F16),
            ("cmask", [P, 8], F16),
            ("norm2", [P, N, 2], F32),
        ):
            a[name] = ctx.enter_context(nc.sbuf_tensor("c_" + name, shape, dt))
        a["ws"] = nc.dram_tensor("ws", (65536,), F32, kind="Internal").ap()
        a["xs"] = nc.dram_tensor("xs", (N * C * HW * HW,), F32, kind="Internal").ap()
        a["Y1"] = nc.dram_tensor("Y1", (2 * Y1N,), F16, kind="Internal").ap()
        a["Gd"] = nc.dram_tensor("Gd", (2 * GDN,), F16, kind="Internal").ap()
        with ExitStack() as early:
            for name, shape, dt in (
                ("Wc", [P, 2, 12, 128], F16),
                ("ident", [P, 128], F32),
                ("gmask", [P, 128], F32),
            ):
                a[name] = early.enter_context(nc.sbuf_tensor("c_" + name, shape, dt))
            stage0(nc, a)
            stage1(nc, a, N)
        stage2(nc, a, N)



def _tile_order():
    return [(2 * ih + il, 2 * jh + jl) for ih in range(2) for jh in range(2) for il in range(2) for jl in range(2)]


def _basis():
    r, w = np.meshgrid(np.arange(16) + 0.5, np.arange(16) + 0.5, indexing="ij")
    even, odd = [], []
    for ky in range(9):
        for kx in range(16):
            if ky in (0, 8) and kx > 8:
                continue
            arg = 2 * np.pi * (kx * r + ky * w) / 16
            other = (16 - kx) % 16 if ky in (0, 8) else kx
            for fs, f in ((even, np.cos(arg)), (odd, np.sin(arg))):
                norm = np.sqrt((f * f).sum())
                if norm > 1e-6:
                    fs.append((f / norm * 4, kx * 9 + ky, other * 9 + ky))
    phi, pos, neg = zip(*(even + odd))
    return np.array(phi), np.array(pos), np.array(neg)


def _split(v):
    hi = v.astype(np.float16)
    return np.stack([hi, (v - hi.astype(np.float64)).astype(np.float16)])


def _layouts(x, L0_conv_gates, L1_conv_w_in, L1_conv_fft_w, L1_conv_w1, L1_conv_w3, L1_conv_w5, L1_conv_w_out):
    N = x.shape[0]
    perm = np.arange(C).reshape(2, 2, 16).transpose(1, 0, 2).reshape(-1)
    d = {}
    d["x"] = np.ascontiguousarray(x[:, perm]).reshape(-1)
    gates = np.asarray(L0_conv_gates).reshape(3, 15, 4, 4)
    row = np.arange(256).reshape(2, P)
    pair = np.stack([(row >> s) & 3 for s in (6, 4, 2, 0)])
    gi = np.arange(4)[:, None, None]
    d["ge"] = np.stack([gates[:, gi + 4 * op, pair] for op in range(2)], 1).transpose(4, 0, 1, 3, 2, 5)
    p = np.arange(P)
    mid = np.stack([(p >> s) & 3 for s in (5, 3, 1)])
    g3 = np.arange(3)[:, None]
    d["go"] = np.concatenate([gates[:, 8 + g3, mid], gates[:, 12 + g3, mid]], 1).transpose(2, 0, 1, 3)
    cross = gates[:, 11].reshape(3, 2, 2, 2, 2)[:, p & 1]
    d["gx"] = cross.transpose(1, 0, 2, 4, 3)
    d["i2"] = (p[:, None] & 1 == np.arange(2)).astype(np.float32)
    d["d_ident"] = np.eye(P, dtype=np.float32)
    grp = (p % C) // 2
    d["d_gmask"] = (grp[:, None] == grp[None]).astype(np.float32) / 4
    d["d_id16"] = np.eye(P, dtype=np.float16)
    d["d_cmask"] = (p[:, None] % 8 == np.arange(8)).astype(np.float16)
    order = _tile_order()
    oi = np.array([o[0] for o in order])
    oj = np.array([o[1] for o in order])
    q = np.arange(4)
    dh = 4 * (q // 2)[None, :, None] + oi[:, None, None] - ((oi + 2) % 4)[None, None, :]
    dw = 4 * (q % 2)[None, :, None] + oj[:, None, None] - ((oj + 2) % 4)[None, None, :]
    def taps(w, size, shift):
        w = np.pad(np.asarray(w).reshape(HID, size, size), ((0, 0), (4, 4), (4, 4)))
        return w[:, dh - shift + 4, dw - shift + 4]
    tab = np.stack([taps(L1_conv_w3, 3, 1), taps(L1_conv_w5, 5, 0)], 2)
    d["tab"] = tab.reshape(NG, 8, 16, 128).transpose(2, 1, 0, 3).reshape(P, NG, 128)
    w1 = np.asarray(L1_conv_w1).reshape(HID)
    d["w1c"] = w1.reshape(KC, C)[:, p % C].T
    d["d_w1g"] = w1.reshape(NG, 8)[:, p % 8].T
    d["win"] = np.asarray(L1_conv_w_in).reshape(HID, C)[:, perm].T.reshape(-1)
    d["wout"] = np.asarray(L1_conv_w_out).reshape(C, 3 * HID)[perm].T.reshape(-1)
    phi, pos, neg = _basis()
    fw = np.asarray(L1_conv_fft_w).reshape(HID, 144)
    d["fw"] = np.stack([fw[:, pos], fw[:, neg]]).reshape(2, HID, 2, P).transpose(3, 2, 0, 1)
    d["d_Bf"] = _split(phi.reshape(2, P, 256)[:, :, :P].transpose(2, 0, 1)).transpose(1, 0, 2, 3)
    tiles = phi.reshape(256, 4, 4, 4, 4)[:, :, oi, :, :]
    tiles = tiles[:, :, np.arange(16), :, oj]
    d["d_Bi"] = _split(tiles.transpose(1, 0, 2, 3)[:, :, :2].reshape(2, P, 128).transpose(1, 0, 2)).transpose(1, 0, 2, 3)
    return {k: np.ascontiguousarray(v) for k, v in d.items()}, perm, N


def kernel(x, L0_conv_gates, L1_conv_w_in, L1_conv_fft_w, L1_conv_w1, L1_conv_w3, L1_conv_w5, L1_conv_w_out):
    import concourse.bacc as bacc
    from concourse.bass_utils import run_bass_kernel_spmd

    arrays, perm, N = _layouts(x, L0_conv_gates, L1_conv_w_in, L1_conv_fft_w, L1_conv_w1, L1_conv_w3, L1_conv_w5, L1_conv_w_out)
    nc = bacc.Bacc("TRN2", target_bir_lowering=False, num_devices=1)
    a = {k: nc.dram_tensor("in_" + k, v.shape, mybir.dt.from_np(v.dtype), kind="ExternalInput").ap() for k, v in arrays.items()}
    a["out"] = nc.dram_tensor("out_dram", (N * C * HW * HW,), F32, kind="ExternalOutput").ap()
    program(nc, a, N)
    r = run_bass_kernel_spmd(nc, [{"in_" + k: v for k, v in arrays.items()}], core_ids=[0])
    out = r.results[0]["out_dram"].reshape(N, C, HW, HW)
    return out[:, np.argsort(perm)]
```
